# Optimizing a Trainium2 kernel written in Bass

```python
import numpy as np
import jax
import jax.numpy as jnp

def _softmax(x, axis=-1):
    return jax.nn.softmax(x, axis=axis)

def _gelu(x):
    return jax.nn.gelu(x, approximate=True)

def _silu(x):
    return jax.nn.silu(x)

def _sigmoid(x):
    return jax.nn.sigmoid(x)

def _layernorm(x, axis=-1, eps=1e-05):
    m = jnp.mean(x, axis=axis, keepdims=True)
    v = jnp.var(x, axis=axis, keepdims=True)
    return (x - m) / jnp.sqrt(v + eps)

def _scatter_add(tgt, idx, src, axis=0):
    return tgt.at[idx].add(src)

def _segment_sum(src, seg, n):
    return jax.ops.segment_sum(src, seg, n)
kernel_name = 'mk_flamingo_gated_d4_seqx_r4_fb82c4'

def setup_inputs(seed: int=0):
    np.random.seed(seed)
    _w = jnp.asarray

    def _rec_inputs():
        import jax
        import jax.numpy as jnp
        _rk = jax.random.key(seed)
        x = -0.0002928 + 1 * jax.random.normal(jax.random.fold_in(_rk, 1), (16, 100, 256), jnp.float32)
        _lenS = 100 - jax.random.randint(jax.random.fold_in(_rk, 7), (16,), 0, max(1, 100 // 4) + 1, jnp.int32)
        _lenS2 = 361 - jax.random.randint(jax.random.fold_in(_rk, 8), (16,), 0, max(1, 361 // 4) + 1, jnp.int32)
        _ctx_1024P = jax.random.normal(jax.random.fold_in(_rk, 11), (16, 16, 256), jnp.float32)
        _ctx_1024c = jax.random.dirichlet(jax.random.fold_in(_rk, 511), 0.3 * jnp.ones((16,), jnp.float32), (16, 361))
        _ctx_1024t = jnp.einsum('bsk,bkd->bsd', _ctx_1024c, _ctx_1024P)
        _ctx_1024t = _ctx_1024t * jax.lax.rsqrt(jnp.mean(jnp.square(_ctx_1024t)) + 1e-12) * 0.953939
        ctx_1024 = -1.52775e-05 + 0.999936 * (_ctx_1024t + 0.3 * jax.random.normal(jax.random.fold_in(_rk, 611), (16, 361, 256), jnp.float32))
        _validS = jnp.arange(100)[None, :] < _lenS[:, None]
        _validS2 = jnp.arange(361)[None, :] < _lenS2[:, None]
        _causal = jnp.tril(jnp.ones((100, 100), dtype=bool))
        mask_BxS2_bk0 = jnp.logical_not(jnp.broadcast_to(_validS2[:, :], (16, 361)))
        mask_BxS_bk0 = jnp.logical_not(jnp.broadcast_to(_validS[:, :], (16, 100)))
        _g = jax.random.normal(jax.random.fold_in(_rk, 9001), (2, 4), jnp.float32)
        _g = jnp.sign(_g) * jnp.maximum(jnp.abs(_g), 1.0) + (_g == 0) * 1.0
        g_xattn = _g[0]
        g_ffn = _g[1]
        return (x, ctx_1024, mask_BxS2_bk0, mask_BxS_bk0, g_xattn, g_ffn)
    x, ctx_1024, mask_BxS2_bk0, mask_BxS_bk0, g_xattn, g_ffn = _rec_inputs()

    def _L0_xattn_setup():
        import jax, jax.numpy as jnp
        import numpy as np
        B, N_TXT, N_IMG, DIM = (8, 128, 1024, 256)
        HEADS, DIM_HEAD = (16, 64)
        INNER = HEADS * DIM_HEAD
        key = jax.random.key(seed)
        ks = jax.random.split(key, 8)
        txt = jax.random.normal(ks[0], (B, N_TXT, DIM), dtype=jnp.float32)
        image = jax.random.normal(ks[1], (B, N_IMG, DIM), dtype=jnp.float32)
        kv_mask = jax.random.randint(ks[2], (B, N_IMG), 0, 2).astype(bool)
        q_mask = jax.random.randint(ks[3], (B, N_TXT), 0, 2).astype(bool)
        s = 0.02
        Wq = jax.random.normal(ks[4], (DIM, INNER), dtype=jnp.float32) * s
        Wkv = jax.random.normal(ks[5], (DIM, 2 * INNER), dtype=jnp.float32) * s
        Wout = jax.random.normal(ks[6], (INNER, DIM), dtype=jnp.float32) * s
        bout = jnp.zeros((DIM,), dtype=jnp.float32)
        return {'txt': txt, 'image': image, 'kv_mask': kv_mask, 'q_mask': q_mask, 'Wq': Wq, 'Wkv': Wkv, 'Wout': Wout, 'bout': bout}
    _L0_xattn_all = _L0_xattn_setup()
    _L0_xattn_in = {k: v for k, v in _L0_xattn_all.items() if k in ('Wq', 'Wkv', 'Wout', 'bout')}
    del _L0_xattn_all

    def _L0_ffn_setup():
        import jax, jax.numpy as jnp
        import numpy as np
        E, TOP_K, D, H = (8, 2, 256, 512)
        B, S = (2, 512)
        key = jax.random.key(seed)
        ks = jax.random.split(key, 10)
        s = 0.02
        return {'x': jax.random.normal(ks[0], (B, S, D), dtype=jnp.float32), 'gate_w': jax.random.normal(ks[1], (E, D), dtype=jnp.float32) * s, 'gate_b': jnp.zeros((E,), dtype=jnp.float32), 'w0': jax.random.normal(ks[2], (E, H, D), dtype=jnp.float32) * s, 'b0': jnp.zeros((E, H), dtype=jnp.float32), 'w1': jax.random.normal(ks[3], (E, H, D), dtype=jnp.float32) * s, 'b1': jnp.zeros((E, H), dtype=jnp.float32), 'w2': jax.random.normal(ks[4], (E, D, H), dtype=jnp.float32) * s, 'b2': jnp.zeros((E, D), dtype=jnp.float32)}
    _L0_ffn_all = _L0_ffn_setup()
    _L0_ffn_in = {k: v for k, v in _L0_ffn_all.items() if k in ('gate_w', 'gate_b', 'w0', 'b0', 'w1', 'b1', 'w2', 'b2')}
    del _L0_ffn_all

    def _L1_xattn_setup():
        import jax, jax.numpy as jnp
        import numpy as np
        import math
        HEADS = 16
        D_MODEL = 256
        D_K = D_MODEL // HEADS
        key = jax.random.key(seed)
        ks = jax.random.split(key, 11)
        B, S = (2, 512)
        s = 1.0 / math.sqrt(D_MODEL)
        return {'q': jax.random.normal(ks[0], (B, S, D_MODEL), jnp.float32), 'k': jax.random.normal(ks[1], (B, S, D_MODEL), jnp.float32), 'v': jax.random.normal(ks[2], (B, S, D_MODEL), jnp.float32), 'Wq': jax.random.normal(ks[3], (D_MODEL, D_MODEL), jnp.float32) * s, 'bq': jax.random.normal(ks[4], (D_MODEL,), jnp.float32) * s, 'Wk': jax.random.normal(ks[5], (D_MODEL, D_MODEL), jnp.float32) * s, 'bk': jax.random.normal(ks[6], (D_MODEL,), jnp.float32) * s, 'Wv': jax.random.normal(ks[7], (D_MODEL, D_MODEL), jnp.float32) * s, 'bv': jax.random.normal(ks[8], (D_MODEL,), jnp.float32) * s, 'Wo': jax.random.normal(ks[9], (D_MODEL, D_MODEL), jnp.float32) * s, 'bo': jax.random.normal(ks[10], (D_MODEL,), jnp.float32) * s}
    _L1_xattn_all = _L1_xattn_setup()
    _L1_xattn_in = {k: v for k, v in _L1_xattn_all.items() if k in ('Wq', 'bq', 'Wk', 'bk', 'Wv', 'bv', 'Wo', 'bo')}
    del _L1_xattn_all

    def _L1_ffn_setup():
        import jax, jax.numpy as jnp
        import numpy as np
        B, S, D, H, O, E, K = (4, 512, 256, 512, 256, 8, 2)
        key = jax.random.key(seed)
        ks = jax.random.split(key, 8)
        x = jax.random.normal(ks[0], (B, S, D), dtype=jnp.float32)
        gate_w = jax.random.uniform(ks[1], (E, D), dtype=jnp.float32, minval=-1, maxval=1) * np.sqrt(6.0 / D)
        gate_b = jnp.zeros((E,), dtype=jnp.float32)
        w1 = jax.random.uniform(ks[2], (E, D, H), dtype=jnp.float32, minval=-1, maxval=1) * np.sqrt(6.0 / D)
        b1 = jnp.zeros((E, H), dtype=jnp.float32)
        w2 = jax.random.uniform(ks[3], (E, H, O), dtype=jnp.float32, minval=-1, maxval=1) * np.sqrt(6.0 / H)
        b2 = jnp.zeros((E, O), dtype=jnp.float32)
        return {'x': x, 'gate_w': gate_w, 'gate_b': gate_b, 'w1': w1, 'b1': b1, 'w2': w2, 'b2': b2}
    _L1_ffn_all = _L1_ffn_setup()
    _L1_ffn_in = {k: v for k, v in _L1_ffn_all.items() if k in ('gate_w', 'gate_b', 'w1', 'b1', 'w2', 'b2')}
    del _L1_ffn_all

    def _L2_xattn_setup():
        import jax, jax.numpy as jnp
        import numpy as np
        B, N, IN_DIM, D_MODEL, H = (4, 512, 256, 256, 16)
        HD = D_MODEL // H
        EPS = 1e-06

        def rope(x):
            n, hd = (x.shape[1], x.shape[3])
            inv_freq = 1.0 / 10000.0 ** (jnp.arange(0, hd, 2, dtype=jnp.float32) / hd)
            ang = jnp.arange(n, dtype=jnp.float32)[:, None] * inv_freq[None, :]
            cos = jnp.cos(ang)[None, :, None, :]
            sin = jnp.sin(ang)[None, :, None, :]
            x1, x2 = (x[..., :hd // 2], x[..., hd // 2:])
            return jnp.concatenate([x1 * cos - x2 * sin, x2 * cos + x1 * sin], axis=-1)

        def rmsnorm(x, w):
            ms = jnp.mean(jnp.square(x), axis=-1, keepdims=True)
            return x * jax.lax.rsqrt(ms + EPS) * w
        key = jax.random.key(seed)
        ks = jax.random.split(key, 12)
        s_in = 1.0 / np.sqrt(IN_DIM)
        s_dm = 1.0 / np.sqrt(D_MODEL)
        return {'q': jax.random.normal(ks[0], (B, N, IN_DIM), jnp.float32), 'k': jax.random.normal(ks[1], (B, N, IN_DIM), jnp.float32), 'v': jax.random.normal(ks[2], (B, N, IN_DIM), jnp.float32), 'wq_w': jax.random.uniform(ks[3], (IN_DIM, D_MODEL), jnp.float32, -s_in, s_in), 'wq_b': jnp.zeros((D_MODEL,), jnp.float32), 'wk_w': jax.random.uniform(ks[4], (IN_DIM, D_MODEL), jnp.float32, -s_in, s_in), 'wk_b': jnp.zeros((D_MODEL,), jnp.float32), 'wv_w': jax.random.uniform(ks[5], (IN_DIM, D_MODEL), jnp.float32, -s_in, s_in), 'wv_b': jnp.zeros((D_MODEL,), jnp.float32), 'wo_w': jax.random.uniform(ks[6], (D_MODEL, IN_DIM), jnp.float32, -s_dm, s_dm), 'wo_b': jnp.zeros((IN_DIM,), jnp.float32), 'qn_w': jnp.ones((HD,), jnp.float32), 'kn_w': jnp.ones((HD,), jnp.float32)}
    _L2_xattn_all = _L2_xattn_setup()
    _L2_xattn_in = {k: v for k, v in _L2_xattn_all.items() if k in ('wq_w', 'wq_b', 'wk_w', 'wk_b', 'wv_w', 'wv_b', 'wo_w', 'wo_b', 'qn_w', 'kn_w')}
    del _L2_xattn_all

    def _L2_ffn_setup():
        import jax, jax.numpy as jnp
        import numpy as np
        SL, BS, HS, FF, E, TOPK = (512, 2, 256, 1024, 8, 2)
        key = jax.random.key(seed)
        ks = jax.random.split(key, 6)
        T = SL * BS
        x = jax.random.normal(ks[0], (SL, BS, HS), jnp.float32)
        scores = jax.random.uniform(ks[1], (T, E), jnp.float32)
        expert_weights = jax.random.uniform(ks[2], (T, TOPK), jnp.float32)
        expert_indices = jax.random.randint(ks[3], (T, TOPK), 0, E, jnp.int32)
        w1 = jax.random.normal(ks[4], (E, HS, FF), jnp.float32) * (1.0 / np.sqrt(HS))
        w2 = jax.random.normal(ks[5], (E, FF, HS), jnp.float32) * (1.0 / np.sqrt(FF))
        bias = jnp.zeros((HS,), jnp.float32)
        return dict(x=x, scores=scores, expert_weights=expert_weights, expert_indices=expert_indices, w1=w1, w2=w2, bias=bias)
    _L2_ffn_all = _L2_ffn_setup()
    _L2_ffn_in = {k: v for k, v in _L2_ffn_all.items() if k in ('scores', 'expert_weights', 'expert_indices', 'w1', 'w2', 'bias')}
    del _L2_ffn_all

    def _L3_xattn_setup():
        import jax, jax.numpy as jnp
        import numpy as np
        D_MODEL = 256
        NUM_HEADS = 16
        HEAD_DIM = D_MODEL // NUM_HEADS
        B, S = (4, 512)
        key = jax.random.key(seed)
        ks = jax.random.split(key, 11)
        scale = 1.0 / np.sqrt(D_MODEL)
        return {'query': jax.random.normal(ks[0], (B, S, D_MODEL), jnp.float32), 'key': jax.random.normal(ks[1], (B, S, D_MODEL), jnp.float32), 'value': jax.random.normal(ks[2], (B, S, D_MODEL), jnp.float32), 'Wq': jax.random.normal(ks[3], (D_MODEL, D_MODEL), jnp.float32) * scale, 'bq': jnp.zeros((D_MODEL,), jnp.float32), 'Wk': jax.random.normal(ks[4], (D_MODEL, D_MODEL), jnp.float32) * scale, 'bk': jnp.zeros((D_MODEL,), jnp.float32), 'Wv': jax.random.normal(ks[5], (D_MODEL, D_MODEL), jnp.float32) * scale, 'bv': jnp.zeros((D_MODEL,), jnp.float32), 'Wo': jax.random.normal(ks[6], (D_MODEL, D_MODEL), jnp.float32) * scale, 'bo': jnp.zeros((D_MODEL,), jnp.float32)}
    _L3_xattn_all = _L3_xattn_setup()
    _L3_xattn_in = {k: v for k, v in _L3_xattn_all.items() if k in ('Wq', 'bq', 'Wk', 'bk', 'Wv', 'bv', 'Wo', 'bo')}
    del _L3_xattn_all

    def _L3_ffn_setup():
        import jax, jax.numpy as jnp
        import numpy as np
        CAPACITY_FACTOR = 1.0

        def _route(token_inputs, Wg, capacity):
            dt = token_inputs.dtype
            logits = jnp.einsum('bnd,de->bne', token_inputs, Wg)
            gates = jax.nn.softmax(logits, axis=-1)
            expert_idx = jnp.argmax(gates, axis=-1)
            mask = jax.nn.one_hot(expert_idx, Wg.shape[1], dtype=dt)
            gate = jnp.sum(gates * mask, axis=-1)
            pos = jnp.cumsum(mask, axis=1) * mask - mask
            keep = mask * (pos < capacity).astype(dt)
            pos_oh = jax.nn.one_hot(pos.astype(jnp.int32), capacity, dtype=dt)
            dispatch = keep[..., None] * pos_oh
            combine = dispatch * gate[:, :, None, None]
            return (dispatch, combine)
        key = jax.random.key(seed)
        k1, k2, k3, k4 = jax.random.split(key, 4)
        B, N, D, E, H = (8, 512, 256, 8, 1024)
        return {'token_inputs': jax.random.normal(k1, (B, N, D), dtype=jnp.float32), 'Wg': jax.random.normal(k2, (D, E), dtype=jnp.float32) * 0.02, 'W1': jax.random.normal(k3, (E, D, H), dtype=jnp.float32) * 0.02, 'W2': jax.random.normal(k4, (E, H, D), dtype=jnp.float32) * 0.02}
    _L3_ffn_all = _L3_ffn_setup()
    _L3_ffn_in = {k: v for k, v in _L3_ffn_all.items() if k in ('Wg', 'W1', 'W2')}
    del _L3_ffn_all
    return {'x': x, 'ctx_1024': ctx_1024, 'mask_BxS2_bk0': mask_BxS2_bk0, 'mask_BxS_bk0': mask_BxS_bk0, 'g_xattn': g_xattn, 'g_ffn': g_ffn, 'L0_xattn_Wq': _L0_xattn_in['Wq'], 'L0_xattn_Wkv': _L0_xattn_in['Wkv'], 'L0_xattn_Wout': _L0_xattn_in['Wout'], 'L0_xattn_bout': _L0_xattn_in['bout'], 'L0_ffn_gate_w': _L0_ffn_in['gate_w'], 'L0_ffn_gate_b': _L0_ffn_in['gate_b'], 'L0_ffn_w0': _L0_ffn_in['w0'], 'L0_ffn_b0': _L0_ffn_in['b0'], 'L0_ffn_w1': _L0_ffn_in['w1'], 'L0_ffn_b1': _L0_ffn_in['b1'], 'L0_ffn_w2': _L0_ffn_in['w2'], 'L0_ffn_b2': _L0_ffn_in['b2'], 'L1_xattn_Wq': _L1_xattn_in['Wq'], 'L1_xattn_bq': _L1_xattn_in['bq'], 'L1_xattn_Wk': _L1_xattn_in['Wk'], 'L1_xattn_bk': _L1_xattn_in['bk'], 'L1_xattn_Wv': _L1_xattn_in['Wv'], 'L1_xattn_bv': _L1_xattn_in['bv'], 'L1_xattn_Wo': _L1_xattn_in['Wo'], 'L1_xattn_bo': _L1_xattn_in['bo'], 'L1_ffn_gate_w': _L1_ffn_in['gate_w'], 'L1_ffn_gate_b': _L1_ffn_in['gate_b'], 'L1_ffn_w1': _L1_ffn_in['w1'], 'L1_ffn_b1': _L1_ffn_in['b1'], 'L1_ffn_w2': _L1_ffn_in['w2'], 'L1_ffn_b2': _L1_ffn_in['b2'], 'L2_xattn_wq_w': _L2_xattn_in['wq_w'], 'L2_xattn_wq_b': _L2_xattn_in['wq_b'], 'L2_xattn_wk_w': _L2_xattn_in['wk_w'], 'L2_xattn_wk_b': _L2_xattn_in['wk_b'], 'L2_xattn_wv_w': _L2_xattn_in['wv_w'], 'L2_xattn_wv_b': _L2_xattn_in['wv_b'], 'L2_xattn_wo_w': _L2_xattn_in['wo_w'], 'L2_xattn_wo_b': _L2_xattn_in['wo_b'], 'L2_xattn_qn_w': _L2_xattn_in['qn_w'], 'L2_xattn_kn_w': _L2_xattn_in['kn_w'], 'L2_ffn_scores': _L2_ffn_in['scores'], 'L2_ffn_expert_weights': _L2_ffn_in['expert_weights'], 'L2_ffn_expert_indices': _L2_ffn_in['expert_indices'], 'L2_ffn_w1': _L2_ffn_in['w1'], 'L2_ffn_w2': _L2_ffn_in['w2'], 'L2_ffn_bias': _L2_ffn_in['bias'], 'L3_xattn_Wq': _L3_xattn_in['Wq'], 'L3_xattn_bq': _L3_xattn_in['bq'], 'L3_xattn_Wk': _L3_xattn_in['Wk'], 'L3_xattn_bk': _L3_xattn_in['bk'], 'L3_xattn_Wv': _L3_xattn_in['Wv'], 'L3_xattn_bv': _L3_xattn_in['bv'], 'L3_xattn_Wo': _L3_xattn_in['Wo'], 'L3_xattn_bo': _L3_xattn_in['bo'], 'L3_ffn_Wg': _L3_ffn_in['Wg'], 'L3_ffn_W1': _L3_ffn_in['W1'], 'L3_ffn_W2': _L3_ffn_in['W2']}

def reference(x, ctx_1024, mask_BxS2_bk0, mask_BxS_bk0, g_xattn, g_ffn, L0_xattn_Wq, L0_xattn_Wkv, L0_xattn_Wout, L0_xattn_bout, L0_ffn_gate_w, L0_ffn_gate_b, L0_ffn_w0, L0_ffn_b0, L0_ffn_w1, L0_ffn_b1, L0_ffn_w2, L0_ffn_b2, L1_xattn_Wq, L1_xattn_bq, L1_xattn_Wk, L1_xattn_bk, L1_xattn_Wv, L1_xattn_bv, L1_xattn_Wo, L1_xattn_bo, L1_ffn_gate_w, L1_ffn_gate_b, L1_ffn_w1, L1_ffn_b1, L1_ffn_w2, L1_ffn_b2, L2_xattn_wq_w, L2_xattn_wq_b, L2_xattn_wk_w, L2_xattn_wk_b, L2_xattn_wv_w, L2_xattn_wv_b, L2_xattn_wo_w, L2_xattn_wo_b, L2_xattn_qn_w, L2_xattn_kn_w, L2_ffn_scores, L2_ffn_expert_weights, L2_ffn_expert_indices, L2_ffn_w1, L2_ffn_w2, L2_ffn_bias, L3_xattn_Wq, L3_xattn_bq, L3_xattn_Wk, L3_xattn_bk, L3_xattn_Wv, L3_xattn_bv, L3_xattn_Wo, L3_xattn_bo, L3_ffn_Wg, L3_ffn_W1, L3_ffn_W2):
    import jax
    import jax.numpy as jnp

    def _L0_xattn_ref(txt, image, kv_mask, q_mask, Wq, Wkv, Wout, bout):
        import jax, jax.numpy as jnp
        import numpy as np
        B, N_TXT, N_IMG, DIM = (8, 128, 1024, 256)
        HEADS, DIM_HEAD = (16, 64)
        INNER = HEADS * DIM_HEAD
        h, d = (HEADS, DIM_HEAD)
        scale = d ** (-0.5)
        b, n2, _ = txt.shape
        n1 = image.shape[1]
        q = (txt @ Wq).reshape(b, n2, h, d).transpose(0, 2, 1, 3)
        kv = image @ Wkv
        k, v = jnp.split(kv, 2, axis=-1)
        k = k.reshape(b, n1, h, d).transpose(0, 2, 1, 3)
        v = v.reshape(b, n1, h, d).transpose(0, 2, 1, 3)
        dots = jnp.einsum('bhid,bhjd->bhij', q, k) * scale
        mask_value = -jnp.finfo(dots.dtype).max
        mask = q_mask[:, None, :, None] & kv_mask[:, None, None, :]
        dots = jnp.where(mask, dots, mask_value)
        attn = jax.nn.softmax(dots, axis=-1)
        out = jnp.einsum('bhij,bhjd->bhid', attn, v)
        out = out.transpose(0, 2, 1, 3).reshape(b, n2, h * d)
        return out @ Wout + bout

    def _L0_ffn_ref(x, gate_w, gate_b, w0, b0, w1, b1, w2, b2):
        import jax, jax.numpy as jnp
        import numpy as np
        E, TOP_K, D, H = (8, 2, 256, 512)
        B, S = (2, 512)
        Bn, Sq, Dv = x.shape
        xt = x.reshape(-1, Dv)
        logits = xt @ gate_w.T + gate_b
        top_v, top_i = jax.lax.top_k(logits, TOP_K)
        h0 = jnp.einsum('td,ehd->eth', xt, w0) + b0[:, None, :]
        h1 = jnp.einsum('td,ehd->eth', xt, w1) + b1[:, None, :]
        act = h0 * jax.nn.silu(h1)
        out_all = jnp.einsum('eth,edh->etd', act, w2) + b2[:, None, :]
        out_te = jnp.transpose(out_all, (1, 0, 2))
        sel = jnp.take_along_axis(out_te, top_i[:, :, None], axis=1)
        w = jax.nn.softmax(top_v, axis=-1)[:, :, None]
        out = (w * sel).sum(axis=1)
        return out.reshape(Bn, Sq, Dv)

    def _L1_xattn_ref(q, k, v, Wq, bq, Wk, bk, Wv, bv, Wo, bo):
        import jax, jax.numpy as jnp
        import numpy as np
        import math
        HEADS = 16
        D_MODEL = 256
        D_K = D_MODEL // HEADS
        B, S, _ = q.shape

        def proj(x, W, b):
            y = x @ W.T + b
            return y.reshape(B, -1, HEADS, D_K).transpose(0, 2, 1, 3)
        qh, kh, vh = (proj(q, Wq, bq), proj(k, Wk, bk), proj(v, Wv, bv))
        scores = jnp.abs(jnp.einsum('bhsd,bhtd->bhst', qh, kh) / math.sqrt(D_K))
        attn = jax.nn.softmax(scores, axis=-1)
        out = jnp.einsum('bhst,bhtd->bhsd', attn, vh)
        concat = out.transpose(0, 2, 1, 3).reshape(B, S, D_MODEL)
        return concat @ Wo.T + bo

    def _L1_ffn_ref(x, gate_w, gate_b, w1, b1, w2, b2):
        import jax, jax.numpy as jnp
        import numpy as np
        B, S, D, H, O, E, K = (4, 512, 256, 512, 256, 8, 2)
        logits = jnp.einsum('bsd,ed->bse', x, gate_w) + gate_b
        probs = jax.nn.softmax(logits, axis=-1)
        topk_vals, topk_idx = jax.lax.top_k(probs, K)
        h = jax.nn.relu(jnp.einsum('bsd,edh->bseh', x, w1) + b1)
        expert_out = jnp.einsum('bseh,eho->bseo', h, w2) + b2
        sel = jnp.take_along_axis(expert_out, topk_idx[..., None], axis=2)
        return jnp.sum(sel * topk_vals[..., None], axis=2)

    def _L2_xattn_ref(q, k, v, wq_w, wq_b, wk_w, wk_b, wv_w, wv_b, wo_w, wo_b, qn_w, kn_w):
        import jax, jax.numpy as jnp
        import numpy as np
        B, N, IN_DIM, D_MODEL, H = (4, 512, 256, 256, 16)
        HD = D_MODEL // H
        EPS = 1e-06

        def rope(x):
            n, hd = (x.shape[1], x.shape[3])
            inv_freq = 1.0 / 10000.0 ** (jnp.arange(0, hd, 2, dtype=jnp.float32) / hd)
            ang = jnp.arange(n, dtype=jnp.float32)[:, None] * inv_freq[None, :]
            cos = jnp.cos(ang)[None, :, None, :]
            sin = jnp.sin(ang)[None, :, None, :]
            x1, x2 = (x[..., :hd // 2], x[..., hd // 2:])
            return jnp.concatenate([x1 * cos - x2 * sin, x2 * cos + x1 * sin], axis=-1)

        def rmsnorm(x, w):
            ms = jnp.mean(jnp.square(x), axis=-1, keepdims=True)
            return x * jax.lax.rsqrt(ms + EPS) * w
        b, nq, _ = q.shape
        nk = k.shape[1]
        qp = (q @ wq_w + wq_b).reshape(b, nq, H, HD)
        kp = (k @ wk_w + wk_b).reshape(b, nk, H, HD)
        vp = (v @ wv_w + wv_b).reshape(b, nk, H, HD).transpose(0, 2, 1, 3)
        qp = rope(qp).transpose(0, 2, 1, 3)
        kp = rope(kp).transpose(0, 2, 1, 3)
        qp = rmsnorm(qp, qn_w)
        kp = rmsnorm(kp, kn_w)
        scale = HD ** (-0.5)
        scores = jnp.einsum('bhqd,bhkd->bhqk', qp, kp) * scale
        attn = jax.nn.softmax(scores, axis=-1)
        out = jnp.einsum('bhqk,bhkd->bhqd', attn, vp)
        out = out.transpose(0, 2, 1, 3).reshape(b, nq, D_MODEL)
        return out @ wo_w + wo_b

    def _L2_ffn_ref(x, scores, expert_weights, expert_indices, w1, w2, bias):
        import jax, jax.numpy as jnp
        import numpy as np
        SL, BS, HS, FF, E, TOPK = (512, 2, 256, 1024, 8, 2)
        sl, bs, hs = x.shape
        n_exp = w1.shape[0]
        top_k = expert_indices.shape[-1]
        xf = x.reshape(-1, hs)
        flat_idx = expert_indices.reshape(-1)
        flat_w = expert_weights.reshape(-1)
        order = jnp.argsort(flat_idx)
        tok = order // top_k
        tokens_per_expert = jnp.bincount(flat_idx, length=n_exp).astype(jnp.int32)
        xs = xf[tok]
        h = jax.nn.gelu(jax.lax.ragged_dot(xs, w1, tokens_per_expert), approximate=False)
        ys = jax.lax.ragged_dot(h, w2, tokens_per_expert)
        ys = ys * flat_w[order][:, None]
        out = jnp.zeros_like(xf).at[tok].add(ys)
        return out.reshape(sl, bs, hs) + bias

    def _L3_xattn_ref(query, key, value, Wq, bq, Wk, bk, Wv, bv, Wo, bo):
        import jax, jax.numpy as jnp
        import numpy as np
        D_MODEL = 256
        NUM_HEADS = 16
        HEAD_DIM = D_MODEL // NUM_HEADS
        B, S = (4, 512)
        b = query.shape[0]

        def split_heads(x):
            return x.reshape(b, -1, NUM_HEADS, HEAD_DIM).transpose(0, 2, 1, 3)
        q = split_heads(query @ Wq.T + bq)
        k = split_heads(key @ Wk.T + bk)
        v = split_heads(value @ Wv.T + bv)
        scores = jnp.einsum('bhqd,bhkd->bhqk', q, k) / np.sqrt(HEAD_DIM)
        weights = jax.nn.softmax(scores, axis=-1)
        out = jnp.einsum('bhqk,bhkd->bhqd', weights, v)
        out = out.transpose(0, 2, 1, 3).reshape(b, -1, D_MODEL)
        return out @ Wo.T + bo

    def _L3_ffn_ref(token_inputs, Wg, W1, W2):
        import jax, jax.numpy as jnp
        import numpy as np
        CAPACITY_FACTOR = 1.0

        def _route(token_inputs, Wg, capacity):
            dt = token_inputs.dtype
            logits = jnp.einsum('bnd,de->bne', token_inputs, Wg)
            gates = jax.nn.softmax(logits, axis=-1)
            expert_idx = jnp.argmax(gates, axis=-1)
            mask = jax.nn.one_hot(expert_idx, Wg.shape[1], dtype=dt)
            gate = jnp.sum(gates * mask, axis=-1)
            pos = jnp.cumsum(mask, axis=1) * mask - mask
            keep = mask * (pos < capacity).astype(dt)
            pos_oh = jax.nn.one_hot(pos.astype(jnp.int32), capacity, dtype=dt)
            dispatch = keep[..., None] * pos_oh
            combine = dispatch * gate[:, :, None, None]
            return (dispatch, combine)
        B, N, D = token_inputs.shape
        E = Wg.shape[1]
        capacity = int(N * CAPACITY_FACTOR // E)
        dispatch, combine = _route(token_inputs, Wg, capacity)
        expert_inputs = jnp.einsum('bnd,bnec->becd', token_inputs, dispatch)
        h = jax.nn.gelu(jnp.einsum('becd,edh->bech', expert_inputs, W1))
        expert_outputs = jnp.einsum('bech,ehd->becd', h, W2)
        output = jnp.einsum('becd,bnec->bnd', expert_outputs, combine)
        return output
    x = x + jnp.tanh(g_xattn[0]) * _L0_xattn_ref(_layernorm(x, axis=-1), ctx_1024, mask_BxS2_bk0, mask_BxS_bk0, L0_xattn_Wq, L0_xattn_Wkv, L0_xattn_Wout, L0_xattn_bout)
    x = x + jnp.tanh(g_ffn[0]) * _L0_ffn_ref(_layernorm(x, axis=-1), L0_ffn_gate_w, L0_ffn_gate_b, L0_ffn_w0, L0_ffn_b0, L0_ffn_w1, L0_ffn_b1, L0_ffn_w2, L0_ffn_b2)
    x = x + jnp.tanh(g_xattn[1]) * _L1_xattn_ref(_layernorm(x, axis=-1), ctx_1024, ctx_1024, L1_xattn_Wq, L1_xattn_bq, L1_xattn_Wk, L1_xattn_bk, L1_xattn_Wv, L1_xattn_bv, L1_xattn_Wo, L1_xattn_bo)
    x = x + jnp.tanh(g_ffn[1]) * _L1_ffn_ref(_layernorm(x, axis=-1), L1_ffn_gate_w, L1_ffn_gate_b, L1_ffn_w1, L1_ffn_b1, L1_ffn_w2, L1_ffn_b2)
    x = x + jnp.tanh(g_xattn[2]) * _L2_xattn_ref(_layernorm(x, axis=-1), ctx_1024, ctx_1024, L2_xattn_wq_w, L2_xattn_wq_b, L2_xattn_wk_w, L2_xattn_wk_b, L2_xattn_wv_w, L2_xattn_wv_b, L2_xattn_wo_w, L2_xattn_wo_b, L2_xattn_qn_w, L2_xattn_kn_w)
    x = x + jnp.tanh(g_ffn[2]) * _L2_ffn_ref(_layernorm(x, axis=-1), L2_ffn_scores, L2_ffn_expert_weights, L2_ffn_expert_indices, L2_ffn_w1, L2_ffn_w2, L2_ffn_bias)
    x = x + jnp.tanh(g_xattn[3]) * _L3_xattn_ref(_layernorm(x, axis=-1), ctx_1024, ctx_1024, L3_xattn_Wq, L3_xattn_bq, L3_xattn_Wk, L3_xattn_bk, L3_xattn_Wv, L3_xattn_bv, L3_xattn_Wo, L3_xattn_bo)
    x = x + jnp.tanh(g_ffn[3]) * _L3_ffn_ref(_layernorm(x, axis=-1), L3_ffn_Wg, L3_ffn_W1, L3_ffn_W2)
    return x

_drawn_inputs = setup_inputs


def setup_inputs(seed=0):
    import zlib

    import numpy as np

    out = dict(_drawn_inputs(seed))
    spreads = {'L0_xattn_bout': (0.0, 0.1),
     'L0_ffn_gate_b': (0.0, 0.1),
     'L0_ffn_b0': (0.0, 0.412),
     'L0_ffn_b1': (0.0, 0.598),
     'L0_ffn_b2': (0.0, 0.1),
     'L1_ffn_gate_b': (0.0, 0.1),
     'L1_ffn_b1': (0.0, 0.1),
     'L1_ffn_b2': (0.0, 0.1),
     'L2_xattn_wq_b': (0.0, 0.8),
     'L2_xattn_wk_b': (0.0, 0.8),
     'L2_xattn_wv_b': (0.0, 0.1),
     'L2_xattn_wo_b': (0.0, 0.1),
     'L2_xattn_qn_w': (1.0, 0.6),
     'L2_xattn_kn_w': (1.0, 0.6),
     'L2_ffn_bias': (0.0, 0.1),
     'L3_xattn_bq': (0.0, 0.683),
     'L3_xattn_bk': (0.0, 2.0),
     'L3_xattn_bv': (0.0, 0.1),
     'L3_xattn_bo': (0.0, 0.1)}
    factors = {'g_ffn': 22.712,
     'L0_xattn_Wq': 8.0,
     'L2_xattn_wq_w': 2.7,
     'L3_ffn_Wg': 5.98,
     'L3_ffn_W1': 5.949,
     'L3_ffn_W2': 5.817}
    for name, (base, spread) in spreads.items():
        noise = np.random.default_rng([zlib.crc32(name.encode()), seed]).standard_normal(out[name].shape)
        drawn = base * np.exp(spread * noise) if base else spread * noise
        out[name] = jnp.asarray(drawn.astype(out[name].dtype))
    for name, factor in factors.items():
        out[name] = (out[name] * factor).astype(out[name].dtype)
    return out
```

```python
from contextlib import ExitStack

import numpy as np
import concourse.bass as bass
from concourse import mybir

F32 = mybir.dt.float32
U8 = mybir.dt.uint8
I32 = mybir.dt.int32
ALU = mybir.AluOpType
ACT = mybir.ActivationFunctionType
AX = mybir.AxisListType

B, S, D = 16, 100, 256
C = 361
KT, KP = 3, 121
CP = KT * KP
KD = D // 128
HEADS = 16
E = 8
CAP = S // E
SLOTS = E * CAP
T2 = 1024
LN_EPS, RMS_EPS = 1e-5, 1e-6
BIG = 1e30


class Signal:

    def __init__(self, sem, per, lead=0):
        self.sem, self.per, self.lead = sem, per, lead

    def at(self, turn, k=0):
        return (turn + self.lead) * self.per + k + 1

    def credit(self, eng):
        eng.sem_inc(self.sem, self.per * self.lead)


def turns(eng, body):
    with eng.Fori(0, B // 2 - 1) as i:
        for par in range(2):
            body(i * 2 + par, par, False)
    body(B - 2, 0, False)
    body(B - 1, 1, True)


def makers(nc, stack):
    def sb(name, shape, dt=F32):
        return stack.enter_context(nc.sbuf_tensor(name, shape, dt))

    def ps(name, shape):
        return stack.enter_context(nc.psum_tensor(name, shape, F32))

    sems = []

    def sem(name):
        sems.append(nc.alloc_semaphore(name))
        return sems[-1]

    def give_back():
        if sems:
            nc.clear_and_free_semaphores(sems)
            nc.all_engine_barrier()

    stack.callback(give_back)
    return sb, ps, sem


def load_state(nc, A, G):
    with ExitStack() as stack:
        sb, ps, sem = makers(nc, stack)
        gates = sb("gates", [128, 8])
        query_mask = sb("query_mask", [S, B], U8)
        any_key = sb("any_key", [S, B])
        state_loaded = sem("state_loaded")
        masks_loaded = sem("masks_loaded")
        tanh_done = sem("tanh_done")
        any_key_done = sem("any_key_done")
        query_on_done = sem("query_on_done")
        block = stack.enter_context(nc.Block())
        loads = [(gates[:, 0:4], A["g_xattn"].partition_broadcast(128)),
                 (gates[:, 4:8], A["g_ffn"].partition_broadcast(128)),
                 (G["x"][:, :, :], A["x"].rearrange("b s d -> s b d")),
                 (G["ident"][:, :], A["ident"]),
                 (G["headmask"][:, :], A["headmask"])]

        @block.sync
        def _(sp):
            sp.dma_start(G["key_mask"][:, :, :], A["mask_BxS2_bk0"].partition_broadcast(S)).then_inc(masks_loaded, 16)
            sp.dma_start(query_mask[:, :], A["mask_BxS_bk0T"]).then_inc(masks_loaded, 16)
            for dst, src in loads:
                sp.dma_start(dst, src).then_inc(state_loaded, 16)
            sp.wait_ge(state_loaded, 16 * len(loads))

        @block.scalar
        def _(act):
            act.wait_ge(state_loaded, 16 * len(loads))
            act.activation(G["tanh"][:, :], gates[:, :], ACT.Tanh).then_inc(tanh_done, 1)

        @block.vector
        def _(dve):
            dve.memset(G["ln_eps"][:, :], LN_EPS)
            dve.memset(G["rms_eps"][:, :], RMS_EPS)
            dve.wait_ge(masks_loaded, 32)
            dve.tensor_reduce(any_key[:, :], G["key_mask"][:, :, :], AX.X, ALU.max).then_inc(any_key_done, 1)
            dve.wait_ge(any_key_done, 1)
            dve.tensor_tensor(G["query_on"][:, :], query_mask[:, :], any_key[:, :], ALU.mult).then_inc(query_on_done, 1)


def layernorm_transposed(nc, G, tag, natural=None, row_scale=None):
    x, xnT, ident = G["x"], G["xnT"], G["ident"]
    R = 4
    with ExitStack() as stack:
        sb, ps, sem = makers(nc, stack)
        stats = sb(f"ln_stats{tag}", [S, B, 6])
        mv = sb(f"ln_mv{tag}", [S, B, 2])
        rstd = sb(f"ln_rstd{tag}", [S, B])
        xn = sb(f"ln_xn{tag}", [S, 2, R, D])
        turned = ps(f"ln_turned_ps{tag}", [128, 2, KD, 512])
        stats_done = sem(f"ln_stats_done{tag}")
        deviation_done = sem(f"ln_deviation_done{tag}")
        rstd_done = sem(f"ln_rstd_done{tag}")
        xn_ready = Signal(sem(f"ln_xn_ready{tag}"), 1)
        turned_ready = Signal(sem(f"ln_turned_ready{tag}"), 1, lead=2)
        xnT_kept = Signal(sem(f"ln_xnT_kept{tag}"), 1, lead=2)
        wait_taken = sem(f"ln_wait_taken{tag}")
        natural_kept = Signal(sem(f"ln_natural_kept{tag}"), 1, lead=2)
        block = stack.enter_context(nc.Block())

        def rounds(eng, body):
            with eng.Fori(0, B // R // 2) as i:
                for par in range(2):
                    body(i * 2 + par, par)

        @block.vector
        def _(dve):
            for b in range(B):
                op = dve.bn_stats(stats[:, b, :], x[:, b, :])
            op.then_inc(stats_done, 1)
            dve.wait_ge(stats_done, 1)
            for b in range(B):
                op = dve.bn_aggr(mv[:, b, :], stats[:, b, :])
            op.then_inc(stats_done, 1)
            dve.wait_ge(deviation_done, 1)
            dve.reciprocal(rstd[:, :], rstd[:, :]).then_inc(rstd_done, 1)
            dve.wait_ge(rstd_done, 1)
            if row_scale is not None:
                dve.tensor_tensor(rstd[:, :], rstd[:, :], row_scale[:, :], ALU.mult).then_inc(rstd_done, 1)
                dve.wait_ge(rstd_done, 2)

            def body(t, par):
                dve.wait_ge(turned_ready.sem, turned_ready.at(t - 2))
                if natural is not None:
                    dve.wait_ge(natural_kept.sem, natural_kept.at(t - 2))
                for r in range(R):
                    op = dve.tensor_scalar(xn[:, par, r:r + 1, :], x[:, bass.ds(t * R + r, 1), :],
                                           mv[:, bass.ds(t * R + r, 1), 0:1].rearrange("p a b -> p (a b)"),
                                           rstd[:, bass.ds(t * R + r, 1)], ALU.subtract, ALU.mult)
                op.then_inc(xn_ready.sem, 1)

            rounds(dve, body)

        @block.tensor
        def _(pe):
            turned_ready.credit(pe)

            def body(t, par):
                pe.wait_ge(xn_ready.sem, xn_ready.at(t))
                pe.wait_ge(xnT_kept.sem, xnT_kept.at(t - 2))
                for r in range(R):
                    for k in range(KD):
                        op = pe.transpose(turned[:, par, k, r * S:(r + 1) * S],
                                          xn[:, par, r, k * 128:(k + 1) * 128], ident[0:S, 0:S])
                op.then_inc(turned_ready.sem, 1)

            rounds(pe, body)

        @block.scalar
        def _(act):
            xnT_kept.credit(act)
            act.wait_ge(stats_done, 2)
            act.activation(rstd[:, :], mv[:, :, 1], ACT.Sqrt, bias=G["ln_eps"][:, 0:1]).then_inc(deviation_done, 1)

            def body(t, par):
                act.wait_ge(turned_ready.sem, turned_ready.at(t))
                act.activation(xnT[:, :, bass.ds(t * R * S, R * S)], turned[:, par, :, 0:R * S],
                               ACT.Copy).then_inc(xnT_kept.sem, 1)

            rounds(act, body)

        if natural is not None:
            @block.gpsimd
            def _(pool):
                natural_kept.credit(pool)

                def body(t, par):
                    pool.wait_ge(xn_ready.sem, xn_ready.at(t))
                    pool.sem_inc(wait_taken, 1)
                    pool.tensor_copy(natural[:, bass.ds(t * R, R), :], xn[:, par, :, :])\
                        .then_inc(natural_kept.sem, 1)

                rounds(pool, body)


class Steps:

    def __init__(self, sem, names, first=()):
        self.sem, self.names = sem, list(names)
        self.first = [n for n in self.names if n in first]
        self.per = len(self.names)

    def credit(self, eng):
        if self.per > len(self.first):
            eng.sem_inc(self.sem, self.per - len(self.first))

    def at(self, turn, name):
        if turn is None:
            return self.per - len(self.first) + self.first.index(name) + 1
        names = self.names
        if isinstance(turn, int) and turn == B - 1:
            names = [n for n in names if n not in self.first]
        return (turn + 1) * self.per + names.index(name) + 1

    def before_turns(self):
        return self.per


def attention(nc, A, G, L):
    DH = 64 if L == 0 else 16
    INNER = HEADS * DH
    M = INNER // 128
    VW = min(512, INNER)
    ROPE = L == 2
    x, xnT, ident, headmask = G["x"], G["xnT"], G["ident"], G["headmask"]
    with ExitStack() as stack:
        sb0, ps0, sem0 = makers(nc, stack)

        def sb(name, shape, dt=F32):
            return sb0(f"a{L}_{name}", shape, dt)

        def signal(name, per, lead=0):
            return Signal(sem0(f"a{L}_{name}"), per, lead)

        wq = sb("wq", [128, KD, INNER])
        wk = sb("wk", [128, KD, INNER])
        wv = sb("wv", [128, KD, INNER])
        wo = sb("wo", [128, M, D])
        bo = sb("bo", [S, D])
        bv = None if L == 0 else sb("bv", [KP, D])
        bqk = sb("bqk", [128, 2, KD]) if L in (1, 3) else None
        if ROPE:
            cos = sb("cos", [KP, KT + 1, DH])
            sin = sb("sin", [KP, KT + 1, DH])
            wqk = sb("wqk", [KP, 2, DH])
            bqk_rows = sb("bqk_rows", [KP, 2, D])
        weights_loaded = sem0(f"a{L}_weights_loaded")
        loads = [(wq[:, :, :], A[f"L{L}_xattn_wq"]), (wk[:, :, :], A[f"L{L}_xattn_wk"]),
                 (wv[:, :, :], A[f"L{L}_xattn_wv"]), (wo[:, :, :], A[f"L{L}_xattn_wo"]),
                 (bo[:, :], A[f"L{L}_xattn_bo"].partition_broadcast(S))]
        if L:
            loads.append((bv[:, :], A[f"L{L}_xattn_bv"].partition_broadcast(KP)))
        if L in (1, 3):
            loads += [(bqk[:, 0, :], A[f"L{L}_xattn_bq"]),
                      (bqk[:, 1, :], A[f"L{L}_xattn_bk"])]
        if ROPE:
            loads += [(cos[:, :, :], A["cos"]), (sin[:, :, :], A["sin"]),
                      (wqk[:, 0, :], A["L2_xattn_qn_w"].partition_broadcast(KP)),
                      (wqk[:, 1, :], A["L2_xattn_kn_w"].partition_broadcast(KP)),
                      (bqk_rows[:, 0, :], A["L2_xattn_wk_b"].partition_broadcast(KP)),
                      (bqk_rows[:, 1, :], A["L2_xattn_wq_b"].partition_broadcast(KP))]
        for dst, src in loads:
            nc.sync.dma_start(dst, src).then_inc(weights_loaded, 16)
        layernorm_transposed(nc, G, f"a{L}", row_scale=G["query_on"] if L == 0 else None)

        ctxT = sb("ctxT", [128, 2, KD, CP])
        qT = sb("qT", [128, 2, M, S])
        qheads = None if L == 0 else sb("qheads", [128, 2, M, 8, S])
        kT = sb("kT", [128, 2, M, CP if ROPE else C])
        v = sb("v", [KP, 2, KT, INNER])
        probs = sb("probs", [S, 4, CP])
        masked = sb("masked", [S, 4, C]) if L == 0 else None
        sizes = sb("sizes", [S, 4, C]) if L == 1 else None
        penalty = sb("penalty", [S, C]) if L == 0 else None
        open_keys = sb("open_keys", [S, C]) if L == 0 else None
        negmax = sb("negmax", [S, HEADS])
        total = sb("total", [S, HEADS])
        scale_out = sb("scale_out", [S, HEADS])
        probsT = sb("probsT", [KP, 2, KT * S])
        attended = sb("attended", [S, INNER])
        attendedT = sb("attendedT", [128, M, S])
        update = sb("update", [S, D])
        ring = ps0(f"a{L}_ring", [128, 4, 512])
        turned = ps0(f"a{L}_turned", [KP, 2, 512])
        mixed = ps0(f"a{L}_mixed", [S, 2, 512])

        ahead = []
        if L == 0:
            ahead += [(f"q{n}", "act") for n in range(2)] + [(f"k{m}", "act") for m in range(M)]
            ahead += [(f"v{n}", "dve") for n in range(6)]
            after, last = [], [("oT0", "act"), ("oT1", "act"), ("out", "dve"), ("pad", None)]
        elif ROPE:
            ahead += [("qn", "dve"), ("kn0", "dve"), ("kn1", "dve"), ("v0", "dve"), ("v1", "dve")]
            after = [("qt", "act"), ("kt0", "act"), ("kt1", "act")]
            last = [("oT0", "act"), ("out", "dve"), ("pad0", None), ("pad1", None)]
        else:
            ahead += [("q0", "act"), ("k0", "act"), ("k1", "act"), ("v0", "dve"), ("v1", "dve")]
            after, last = [], [("oT0", "act"), ("out", "dve"), ("pad", None)]
        heads = [(f"s{h}", "dve" if L == 0 else "act") for h in range(HEADS)]
        units = ahead + heads + after + last
        assert len(units) % 4 == 0, len(units)
        names = [name for name, _ in units]
        owner = dict(units)
        first = {name for name, _ in ahead + after}
        unit_filled = Steps(sem0(f"a{L}_unit_filled"), [n for n in names if owner[n]], first)
        evacuated = {"act": Steps(sem0(f"a{L}_act_evacuated"), [n for n in names if owner[n] == "act"], first),
                     "dve": Steps(sem0(f"a{L}_dve_evacuated"), [n for n in names if owner[n] == "dve"], first)}
        per_head = [f"h{h}" for h in range(HEADS)]
        negmax_ready = Steps(sem0(f"a{L}_negmax_ready"), per_head)
        probs_ready = Steps(sem0(f"a{L}_probs_ready"), per_head) if L == 0 else evacuated["act"]
        probs_turned = Steps(sem0(f"a{L}_probs_turned"), per_head)
        probsT_ready = Steps(sem0(f"a{L}_probsT_ready"), per_head)
        values_mixed = Steps(sem0(f"a{L}_values_mixed"), per_head)
        sizes_ready = Steps(sem0(f"a{L}_sizes_ready"), per_head)
        qheads_ready = Steps(sem0(f"a{L}_qheads_ready"), ["qheads"], ["qheads"])
        penalty_done = Steps(sem0(f"a{L}_penalty_done"), ["open", "penalty"])
        norm_done = Steps(sem0(f"a{L}_norm_done"), ["scale", "attended"])
        update_done = Steps(sem0(f"a{L}_update_done"), ["x"])
        context_loaded = [sem0(f"a{L}_context_loaded{par}") for par in range(2)]
        wait_taken = sem0(f"a{L}_wait_taken")
        setup_done = sem0(f"a{L}_setup_done")
        if ROPE:
            rot = sb("rot", [KP, KT + 1, D])
            rot_c = sb("rot_c", [KP, KT + 1, D])
            rot_s = sb("rot_s", [KP, KT + 1, D])
            squares = sb("squares", [KP, KT + 1, D])
            inv_rms = sb("inv_rms", [KP, (KT + 1) * HEADS])
            xnT_now = sb("xnT_now", [128, KD, KP])
            xnT_copied = Steps(sem0("a2_xnT_copied"), ["copy"], ["copy"])
            rotated = Steps(sem0("a2_rotated"), ["cos", "sin", "sum"], ["cos", "sin", "sum"])
            rooted = Steps(sem0("a2_rooted"), ["root"], ["root"])
            squared = Steps(sem0("a2_squared"), ["sq"], ["sq"])
            rms_done = Steps(sem0("a2_rms_done"), ["sum", "inverse"], ["sum", "inverse"])
            normed = Steps(sem0("a2_normed"), ["unit", "weighted"], ["unit", "weighted"])

        def bank(name):
            return ring[:, names.index(name) % 4, :]

        WEIGHTS = 16 * len(loads)
        SETUP = 2 + (L in (1, 3)) + 2 * ROPE
        block = stack.enter_context(nc.Block())

        @block.sync
        def _(sp):
            def load(b, par):
                sp.dma_start(ctxT[:, par, :, 0:C], A["ctxT"][bass.ds(b, 1), :, :, :])\
                    .then_inc(context_loaded[par], 16)

            load(0, 0)
            load(1, 1)

            last_v = "v5" if L == 0 else "v1"

            def body(t, par):
                sp.wait_ge(unit_filled.sem, unit_filled.at(t - 1, last_v))
                load(t + 2, par)

            sp.wait_ge(unit_filled.sem, unit_filled.at(None, last_v))
            load(2, 0)
            with sp.Fori(0, B // 2 - 2) as i:
                for par in range(2):
                    body(i * 2 + 1 + par, 1 - par)
            body(B - 3, 1)

        @block.tensor
        def _(pe):
            for steps in (unit_filled, probs_turned, values_mixed):
                steps.credit(pe)
            pe.wait_ge(weights_loaded, WEIGHTS)
            pe.wait_ge(setup_done, SETUP)

            def free(t, name):
                n = names.index(name) - 4
                turn = t
                if t is None:
                    known = [m for m in names[:n + 1 if n >= 0 else 0][::-1] if m in first and (names.index(m) - n) % 4 == 0]
                    if known:
                        pe.wait_ge(evacuated[owner[known[0]]].sem, evacuated[owner[known[0]]].at(None, known[0]))
                    return
                while n < 0 or not owner[names[n]] or (isinstance(turn, int) and turn == B - 1 and names[n] in first):
                    if n < 0:
                        n, turn = n + len(names), turn - 1
                    else:
                        n -= 4
                who = evacuated[owner[names[n]]]
                pe.wait_ge(who.sem, who.at(turn, names[n]))

            def project(t, name, parts):
                free(t, name)
                for n, (dst, lhsT, rhs, start, stop) in enumerate(parts):
                    op = pe.matmul(dst, lhsT, rhs, start=start, stop=stop)
                op.then_inc(unit_filled.sem, 1)

            def ahead_of(t, par):
                b = 0 if t is None else t + 1
                pe.wait_ge(context_loaded[par], b * 8 + 16 - 8 * par)
                tokens = slice(0, S) if t is None else bass.ds(b * S, S)
                if ROPE:
                    pe.wait_ge(xnT_copied.sem, xnT_copied.at(t, "copy"))
                    project(t, "qn", [(bank("qn")[0:KP, 0:D], xnT_now[:, k, :], wq[:, k, :], k == 0, k == KD - 1)
                                            for k in range(KD)])
                else:
                    for n in range(2 if L == 0 else 1):
                        project(t, f"q{n}",
                                [(bank(f"q{n}")[:, j * S:(j + 1) * S], wq[:, k, (4 * n + j) * 128:(4 * n + j + 1) * 128],
                                  xnT[:, k, tokens], k == 0, k == KD - 1)
                                 for j in range(min(4, M)) for k in range(KD)])
                    for m in range(M):
                        project(t, f"k{m}",
                                [(bank(f"k{m}")[:, 0:C], wk[:, k, m * 128:(m + 1) * 128], ctxT[:, par, k, 0:C],
                                  k == 0, k == KD - 1) for k in range(KD)])

                def rows(name, kt, c0, width, w, w0):
                    return [(bank(name)[0:KP, c0:c0 + width], ctxT[:, par, k, kt * KP:(kt + 1) * KP],
                             w[:, k, w0:w0 + width], k == 0, k == KD - 1) for k in range(KD)]

                if ROPE:
                    project(t, "kn0", rows("kn0", 0, 0, D, wk, 0) + rows("kn0", 1, D, D, wk, 0))
                    project(t, "kn1", rows("kn1", 2, 0, D, wk, 0))
                if L == 0:
                    for n in range(6):
                        project(t, f"v{n}", rows(f"v{n}", n // 2, 0, 512, wv, (n % 2) * 512))
                else:
                    project(t, "v0", rows("v0", 0, 0, D, wv, 0) + rows("v0", 1, D, D, wv, 0))
                    project(t, "v1", rows("v1", 2, 0, D, wv, 0))

            def turn_rotated(t):
                if not ROPE:
                    return
                pe.wait_ge(normed.sem, normed.at(t, "weighted"))
                free(t, "qt")
                for m in range(M):
                    op = pe.transpose(bank("qt")[:, m * S:(m + 1) * S], rot_c[0:S, KT, m * 128:(m + 1) * 128],
                                      ident[0:S, 0:S])
                op.then_inc(unit_filled.sem, 1)
                for m in range(M):
                    free(t, f"kt{m}")
                    for kt in range(KT):
                        op = pe.transpose(bank(f"kt{m}")[:, kt * KP:(kt + 1) * KP],
                                          rot_c[:, kt, m * 128:(m + 1) * 128], ident[0:KP, 0:KP])
                    op.then_inc(unit_filled.sem, 1)

            def scores(t, par, h):
                if h < 4:
                    free(t, f"s{h}")
                out = bank(f"s{h}")[0:S, 0:C]
                if L == 0:
                    m, p = h // 2, 64 * (h % 2)
                    op = pe.matmul(out, qT[p:p + 64, par, m, :], kT[p:p + 64, par, m, 0:C], start=True, stop=True)
                else:
                    m, j = h // 8, h % 8
                    op = pe.matmul(out, qheads[:, par, m, j, :], kT[:, par, m, 0:C], start=True, stop=True)
                op.then_inc(unit_filled.sem, 1)

            def turn_probs(t, h):
                pe.wait_ge(probs_ready.sem, probs_ready.at(t, f"h{h}" if L == 0 else f"s{h}"))
                for kt in range(KT):
                    op = pe.transpose(turned[:, h % 2, kt * S:(kt + 1) * S], probs[:, h % 4, kt * KP:(kt + 1) * KP],
                                      ident[0:S, 0:S])
                op.then_inc(probs_turned.sem, 1)

            def mix(t, par, h):
                pe.wait_ge(probsT_ready.sem, probsT_ready.at(t, f"h{h}"))
                if h == 0:
                    pe.wait_ge(norm_done.sem, norm_done.at(t - 1, "attended"))
                c0 = h * DH
                for kt in range(KT):
                    op = pe.matmul(mixed[:, c0 // 512, c0 % 512:c0 % 512 + DH], probsT[:, h % 2, kt * S:(kt + 1) * S],
                                   v[:, par, kt, c0:c0 + DH], start=kt == 0, stop=kt == KT - 1)
                op.then_inc(values_mixed.sem, 1)

            def body(t, par, last):
                if not last:
                    ahead_of(t, 1 - par)
                pe.wait_ge(evacuated["dve"].sem, evacuated["dve"].at(t - 1, "v5" if L == 0 else "v1"))
                if L == 0:
                    pe.wait_ge(evacuated["act"].sem, evacuated["act"].at(t - 1, f"k{M - 1}"))
                else:
                    pe.wait_ge(evacuated["act"].sem, evacuated["act"].at(t - 1, "kt1" if ROPE else "k1"))
                    pe.wait_ge(qheads_ready.sem, qheads_ready.at(t - 1, "qheads"))
                for h in range(3):
                    scores(t, par, h)
                for h in range(HEADS):
                    turn_probs(t, h)
                    if h + 3 < HEADS:
                        scores(t, par, h + 3)
                    if h:
                        mix(t, par, h - 1)
                mix(t, par, HEADS - 1)
                if not last:
                    turn_rotated(t)
                pe.wait_ge(norm_done.sem, norm_done.at(t, "attended"))
                for n in range(2 if L == 0 else 1):
                    free(t, f"oT{n}")
                    for j in range(min(4, M)):
                        m = 4 * n + j
                        op = pe.transpose(bank(f"oT{n}")[:, j * S:(j + 1) * S], attended[:, m * 128:(m + 1) * 128],
                                          ident[0:S, 0:S])
                    op.then_inc(unit_filled.sem, 1)
                oT = "oT1" if L == 0 else "oT0"
                pe.wait_ge(evacuated["act"].sem, evacuated["act"].at(t, oT))
                project(t, "out", [(bank("out")[0:S, 0:D], attendedT[:, m, :], wo[:, m, :], m == 0, m == M - 1)
                                         for m in range(M)])

            ahead_of(None, 0)
            turn_rotated(None)
            for steps in evacuated.values():
                pe.wait_ge(steps.sem, steps.before_turns())
            turns(pe, body)

        @block.scalar
        def _(act):
            credits = [evacuated["act"]] + ([probs_ready] if L == 0 else []) + ([sizes_ready] if L == 1 else [])
            for steps in credits + ([xnT_copied, squared, rooted] if ROPE else []):
                steps.credit(act)
            act.wait_ge(weights_loaded, WEIGHTS)
            act.wait_ge(setup_done, SETUP)
            done = evacuated["act"].sem

            def filled(t, name):
                act.wait_ge(unit_filled.sem, unit_filled.at(t, name))

            def ahead_of(t, par):
                b = 0 if t is None else t + 1
                if ROPE:
                    if t is not None:
                        act.wait_ge(unit_filled.sem, unit_filled.at(t - 1, "qn"))
                    act.activation(xnT_now[:, :, 0:S], xnT[:, :, 0:S] if t is None else xnT[:, :, bass.ds(b * S, S)],
                                   ACT.Copy).then_inc(xnT_copied.sem, 1)
                elif L == 0:
                    for n in range(2):
                        filled(t, f"q{n}")
                        act.activation(qT[:, par, 4 * n:4 * n + 4, :], bank(f"q{n}")[:, 0:4 * S],
                                       ACT.Copy, scale=-DH ** -0.5).then_inc(done, 1)
                    for m in range(M):
                        filled(t, f"k{m}")
                        act.activation(kT[:, par, m, :], bank(f"k{m}")[:, 0:C], ACT.Copy).then_inc(done, 1)
                else:
                    filled(t, "q0")
                    for m in range(M):
                        op = act.activation(qT[:, par, m, :], bank("q0")[:, m * S:(m + 1) * S], ACT.Identity,
                                            bias=bqk[:, 0, m:m + 1], scale=DH ** -0.5)
                    op.then_inc(done, 1)
                    for m in range(M):
                        filled(t, f"k{m}")
                        act.activation(kT[:, par, m, :], bank(f"k{m}")[:, 0:C], ACT.Identity,
                                       bias=bqk[:, 1, m:m + 1]).then_inc(done, 1)

            def square(t):
                act.wait_ge(rotated.sem, rotated.at(t, "sum"))
                act.activation(squares[:, :, :], rot[:, :, :], ACT.Square).then_inc(squared.sem, 1)

            def root(t):
                act.wait_ge(rms_done.sem, rms_done.at(t, "sum"))
                act.activation(inv_rms[:, :], inv_rms[:, :], ACT.Sqrt, bias=G["rms_eps"][0:KP, 0:1], scale=1.0 / DH)\
                    .then_inc(rooted.sem, 1)

            def keep_rotated(t, par):
                filled(t, "qt")
                act.activation(qT[:, par, :, :], bank("qt")[:, 0:M * S], ACT.Copy).then_inc(done, 1)
                for m in range(M):
                    filled(t, f"kt{m}")
                    act.activation(kT[:, par, m, :], bank(f"kt{m}")[:, 0:CP], ACT.Copy).then_inc(done, 1)

            def exponentials(t, h):
                if L == 0:
                    act.wait_ge(evacuated["dve"].sem, evacuated["dve"].at(t, f"s{h}"))
                else:
                    act.wait_ge(negmax_ready.sem, negmax_ready.at(t, f"h{h}"))
                if h == 0:
                    act.wait_ge(norm_done.sem, norm_done.at(t - 1, "attended"))
                source, scale = bank(f"s{h}")[0:S, 0:C], 1.0
                if L == 0:
                    source, scale = masked[:, h % 4, :], -1.0
                if L == 1:
                    act.activation(sizes[:, h % 4, :], source, ACT.Abs).then_inc(sizes_ready.sem, 1)
                    act.wait_ge(sizes_ready.sem, sizes_ready.at(t, f"h{h}"))
                    source = sizes[:, h % 4, :]
                act.activation(probs[:, h % 4, 0:C], source, ACT.Exp, bias=negmax[:, h:h + 1], scale=scale,
                               accum_out=total[:, h:h + 1]).then_inc(probs_ready.sem, 1)

            def body(t, par, last):
                if not last:
                    ahead_of(t, 1 - par)
                for h in range(HEADS):
                    exponentials(t, h)
                    if ROPE and not last and h == 8:
                        square(t)
                    if ROPE and not last and h == 11:
                        root(t)
                if ROPE and not last:
                    keep_rotated(t, 1 - par)
                for n in range(2 if L == 0 else 1):
                    filled(t, f"oT{n}")
                    w = min(4, M)
                    act.activation(attendedT[:, w * n:w * n + w, :], bank(f"oT{n}")[:, 0:w * S], ACT.Copy)\
                        .then_inc(done, 1)

            ahead_of(None, 0)
            if ROPE:
                square(None)
                root(None)
                keep_rotated(None, 0)
            turns(act, body)

        @block.vector
        def _(dve):
            for steps in [evacuated["dve"], negmax_ready, probsT_ready, norm_done, update_done, penalty_done] + \
                    ([rms_done] if ROPE else []):
                steps.credit(dve)
            for par in range(2):
                op = dve.memset(ctxT[:, par, :, C:CP], 0.0)
            op.then_inc(setup_done, 1)
            dve.memset(probs[:, :, C:CP], 0.0).then_inc(setup_done, 1)
            dve.wait_ge(weights_loaded, WEIGHTS)
            if L in (1, 3):
                dve.tensor_scalar(bqk[:, 0, :], bqk[:, 0, :], DH ** -0.5, None, ALU.mult).then_inc(setup_done, 1)
            if ROPE:
                dve.memset(xnT_now[:, :, S:KP], 0.0).then_inc(setup_done, 1)
                dve.scalar_tensor_tensor(wqk[:, 0, :], wqk[:, 0, :], DH ** -0.5, wqk[:, 1, :], ALU.mult, ALU.mult)\
                    .then_inc(setup_done, 1)
            done = evacuated["dve"].sem

            def filled(t, name):
                dve.wait_ge(unit_filled.sem, unit_filled.at(t, name))

            def add_rows(dst, src, bias, tiles):
                return dve.tensor_tensor(dst, src.rearrange("p (t d) -> p t d", t=tiles),
                                         bias.unsqueeze(1).broadcast_to([KP, tiles, D]), ALU.add)

            def ahead_of(t, par):
                if ROPE:
                    if t is not None:
                        dve.wait_ge(normed.sem, normed.at(t - 1, "weighted"))
                    filled(t, "qn")
                    add_rows(rot[:, KT:KT + 1, :], bank("qn")[0:KP, 0:D], bqk_rows[:, 1, :], 1).then_inc(done, 1)
                    filled(t, "kn0")
                    add_rows(rot[:, 0:2, :], bank("kn0")[0:KP, 0:2 * D], bqk_rows[:, 0, :], 2).then_inc(done, 1)
                    filled(t, "kn1")
                    add_rows(rot[:, 2:3, :], bank("kn1")[0:KP, 0:D], bqk_rows[:, 0, :], 1).then_inc(done, 1)
                if L == 0:
                    for n in range(6):
                        filled(t, f"v{n}")
                        dve.tensor_copy(v[:, par, n // 2, (n % 2) * 512:(n % 2) * 512 + 512], bank(f"v{n}")[0:KP, :])\
                            .then_inc(done, 1)
                else:
                    filled(t, "v0")
                    add_rows(v[:, par, 0:2, :], bank("v0")[0:KP, 0:2 * D], bv[:, :], 2).then_inc(done, 1)
                    filled(t, "v1")
                    add_rows(v[:, par, 2:3, :], bank("v1")[0:KP, 0:D], bv[:, :], 1).then_inc(done, 1)

            def rms(t):
                dve.wait_ge(squared.sem, squared.at(t, "sq"))
                dve.tensor_reduce(inv_rms[:, :], squares[:, :, :].rearrange("p t (h d) -> p (t h) d", d=DH), AX.X,
                                  ALU.add).then_inc(rms_done.sem, 1)
                dve.wait_ge(rooted.sem, rooted.at(t, "root"))
                dve.reciprocal(inv_rms[:, :], inv_rms[:, :]).then_inc(rms_done.sem, 1)

            def largest(t, h):
                filled(t, f"s{h}")
                source = bank(f"s{h}")[0:S, 0:C]
                if L == 0:
                    dve.sem_inc(wait_taken, 1)
                    op = dve.tensor_tensor_reduce(masked[:, h % 4, :], source, penalty[:, :], 1.0, BIG, ALU.add, ALU.min,
                                                  negmax[:, h:h + 1])
                    op.then_inc(done, 1)
                else:
                    dve.tensor_reduce(negmax[:, h:h + 1], source, AX.X, ALU.max, negate=True,
                                      apply_absolute_value=L == 1).then_inc(negmax_ready.sem, 1)

            def keep_probsT(t, h):
                dve.wait_ge(probs_turned.sem, probs_turned.at(t, f"h{h}"))
                dve.tensor_copy(probsT[:, h % 2, :], turned[:, h % 2, 0:KT * S]).then_inc(probsT_ready.sem, 1)

            def body(t, par, last):
                if not last:
                    ahead_of(t, 1 - par)
                if L == 0:
                    entry = bass.ds(t, 1)
                    dve.wait_ge(evacuated["dve"].sem, evacuated["dve"].at(t - 1, f"s{HEADS - 1}"))
                    dve.tensor_scalar(open_keys[:, :].unsqueeze(1), G["key_mask"][:, entry, :], -BIG, BIG, ALU.mult, ALU.add)\
                        .then_inc(penalty_done.sem, 1)
                    dve.wait_ge(penalty_done.sem, penalty_done.at(t, "open"))
                    dve.tensor_scalar(penalty[:, :], open_keys[:, :], G["query_on"][:, entry], None, ALU.mult)\
                        .then_inc(penalty_done.sem, 1)
                    dve.wait_ge(penalty_done.sem, penalty_done.at(t, "penalty"))
                for h in range(3):
                    largest(t, h)
                for h in range(HEADS):
                    keep_probsT(t, h)
                    if h + 3 < HEADS:
                        largest(t, h + 3)
                    if ROPE and not last and h == 9:
                        rms(t)
                dve.wait_ge(probs_ready.sem, probs_ready.at(t, f"h{HEADS - 1}" if L == 0 else f"s{HEADS - 1}"))
                dve.reciprocal(scale_out[:, :], total[:, :]).then_inc(norm_done.sem, 1)
                dve.wait_ge(norm_done.sem, norm_done.at(t, "scale"))
                dve.wait_ge(values_mixed.sem, values_mixed.at(t, f"h{HEADS - 1}"))
                if L == 0:
                    out, source = attended[:, :], mixed[:, :, :].rearrange("p a n -> p (a n)")
                else:
                    out, source = attended[:, :], mixed[:, 0, 0:INNER]
                dve.tensor_tensor(out.rearrange("p (h d) -> p h d", h=HEADS), source.rearrange("p (h d) -> p h d", h=HEADS),
                                  scale_out[:, :].unsqueeze(2).broadcast_to([S, HEADS, DH]), ALU.mult)\
                    .then_inc(norm_done.sem, 1)
                filled(t, "out")
                dve.wait_ge(update_done.sem, update_done.at(t - 1, "x"))
                dve.tensor_tensor(update[:, :], bank("out")[0:S, 0:D], bo[:, :], ALU.add).then_inc(done, 1)
                dve.wait_ge(evacuated["dve"].sem, evacuated["dve"].at(t, "out"))
                entry = x[:, bass.ds(t, 1), :]
                dve.scalar_tensor_tensor(entry, update[:, :].unsqueeze(1), G["tanh"][0:S, L:L + 1], entry,
                                         ALU.mult, ALU.add).then_inc(update_done.sem, 1)

            ahead_of(None, 0)
            if ROPE:
                rms(None)
            turns(dve, body)

        if L:
            @block.gpsimd
            def _(pool):
                for steps in [qheads_ready] + ([rotated, normed] if ROPE else []):
                    steps.credit(pool)
                pool.wait_ge(weights_loaded, WEIGHTS)
                pool.wait_ge(setup_done, SETUP)

                def spread_heads(t, par):
                    name = "qt" if ROPE else "q0"
                    pool.wait_ge(evacuated["act"].sem, evacuated["act"].at(t, name))
                    pool.tensor_tensor(qheads[:, par, :, :, :],
                                       qT[:, par, :, :].unsqueeze(2).broadcast_to([128, M, 8, S]),
                                       headmask[:, :].unsqueeze(1).unsqueeze(3).broadcast_to([128, M, 8, S]), ALU.mult)\
                        .then_inc(qheads_ready.sem, 1)

                def rotate(t):
                    pool.wait_ge(evacuated["dve"].sem, evacuated["dve"].at(t, "kn1"))
                    wide = [KP, KT + 1, HEADS, DH // 2]

                    def halves(buf):
                        r = buf[:, :, :].rearrange("p t (h a d) -> p t h a d", a=2, d=DH // 2)
                        return r[:, :, :, 0, :], r[:, :, :, 1, :]

                    def table(buf, a):
                        return buf[:, :, a * (DH // 2):(a + 1) * (DH // 2)].unsqueeze(2).broadcast_to(wide)

                    one, two = halves(rot)
                    s_one, s_two = halves(rot_s)
                    c_one, c_two = halves(rot_c)
                    pool.tensor_tensor(c_one, one, table(cos, 0), ALU.mult)
                    pool.tensor_tensor(c_two, two, table(cos, 1), ALU.mult).then_inc(rotated.sem, 1)
                    pool.tensor_tensor(s_one, two, table(sin, 0), ALU.mult)
                    pool.tensor_tensor(s_two, one, table(sin, 1), ALU.mult).then_inc(rotated.sem, 1)
                    pool.wait_ge(rotated.sem, rotated.at(t, "sin"))
                    pool.tensor_tensor(rot[:, :, :], rot_c[:, :, :], rot_s[:, :, :], ALU.add).then_inc(rotated.sem, 1)

                def normalize(t):
                    pool.wait_ge(rms_done.sem, rms_done.at(t, "inverse"))
                    unit = rot_c[:, :, :].rearrange("p t (h d) -> p (t h) d", d=DH)
                    pool.tensor_tensor(unit, rot[:, :, :].rearrange("p t (h d) -> p (t h) d", d=DH),
                                       inv_rms[:, :].unsqueeze(2).broadcast_to([KP, (KT + 1) * HEADS, DH]), ALU.mult)\
                        .then_inc(normed.sem, 1)
                    pool.wait_ge(normed.sem, normed.at(t, "unit"))
                    q = rot_c[:, KT, :].rearrange("p (h d) -> p h d", d=DH)
                    pool.tensor_tensor(q, q, wqk[:, 0, :].unsqueeze(1).broadcast_to([KP, HEADS, DH]), ALU.mult)\
                        .then_inc(normed.sem, 1)

                def ahead_of(t, par):
                    if ROPE:
                        rotate(t)
                        normalize(t)
                    spread_heads(t, par)

                ahead_of(None, 0)

                def body(t, par, last):
                    if not last:
                        ahead_of(t, 1 - par)

                turns(pool, body)


def route(nc, A, G, L, R):
    xnT, ident = G["xnT"], G["ident"]
    with ExitStack() as stack:
        sb0, ps0, sem0 = makers(nc, stack)

        def sb(name, shape, dt=F32):
            return sb0(f"r{L}_{name}", shape, dt)

        def sem(name):
            return sem0(f"r{L}_{name}")

        wide = [S, B, E]
        reverse = sb("reverse", [S, E])
        expert = sb("expert", [S, E])
        logits = sb("logits", wide)
        top = sb("top", [S, B])
        top2 = sb("top2", [S, B])
        equal = sb("equal", wide)
        rank = sb("rank", [S, B])
        first = sb("first", wide)
        second = sb("second", wide)
        share = sb("share", [S, B])
        share2 = sb("share2", [S, B])
        loaded = sem("loaded")
        logits_ready = sem("logits_ready")
        shifted_ready = sem("shifted_ready")
        exp_ready = sem("exp_ready")
        step_done = sem("step_done")
        loads = [(reverse[:, :], A["reverse"].partition_broadcast(S)), (expert[:, :], A["expert"].partition_broadcast(S))]
        if L != 2:
            gate_w = sb("gate_w", [128, KD, E])
            logits_ps = ps0(f"r{L}_logits_ps", [S, B * E])
            loads.append((gate_w[:, :, :], A[f"L{L}_gate_w"]))
        if L < 2:
            gate_b = sb("gate_b", [S, E])
            b2 = sb("b2", [E, D])
            weightT = sb("weightT", [E, 4, 4 * S])
            weightT_ps = ps0(f"r{L}_weightT_ps", [E, 4, 512])
            bias_ps = ps0(f"r{L}_bias_ps", [S, 2, 2 * D])
            weight_ready = sem("weight_ready")
            weightT_ready = sem("weightT_ready")
            weightT_kept = sem("weightT_kept")
            bias_ready = sem("bias_ready")
            bias_added = sem("bias_added")
            loads += [(gate_b[:, :], A[f"L{L}_ffn_gate_b"].partition_broadcast(S)), (b2[:, :], A[f"L{L}_ffn_b2"])]
        if L == 2:
            FULL = T2 // S
            REST = T2 - FULL * S
            chosen = sb("chosen", [S, B, 2], I32)
            chosen_f = sb("chosen_f", [S, B, 2])
            given = sb("given", [S, B, 2])
            bias = sb("bias", [S, D])
            cleared = sem("cleared")
            for dst, name in ((chosen, "L2_indices"), (given, "L2_weights")):
                loads += [(dst[:, 0:FULL, :], A[name][0:FULL * S, :].rearrange("(b s) k -> s b k", s=S)),
                          (dst[0:REST, FULL, :], A[name][FULL * S:T2, :])]
            loads.append((bias[:, :], A["L2_ffn_bias"].partition_broadcast(S)))
        if L == 3:
            upto = sb("upto", [S, S])
            slot = sb("slot", [S, CAP])
            place = sb("place", wide)
            upto_ps = ps0("r3_upto_ps", [S, B * E])
            first_ready = sem("first_ready")
            counted = sem("counted")
            loads += [(upto[:, :], A["upto"]), (slot[:, :], A["slot"].partition_broadcast(S))]
        block = stack.enter_context(nc.Block())

        def over(ap):
            return ap.unsqueeze(2).broadcast_to(wide)

        def rows(ap):
            return ap.unsqueeze(1).broadcast_to(wide)

        @block.sync
        def _(sp):
            if L == 2:
                sp.wait_ge(cleared, 2)
            for dst, src in loads:
                sp.dma_start(dst, src).then_inc(loaded, 16)

        @block.tensor
        def _(pe):
            pe.wait_ge(loaded, 16 * len(loads))
            if L != 2:
                for b in range(B):
                    for k in range(KD):
                        op = pe.matmul(logits_ps[:, b * E:(b + 1) * E], xnT[:, k, b * S:(b + 1) * S], gate_w[:, k, :],
                                       start=k == 0, stop=k == KD - 1)
                op.then_inc(logits_ready, 1)
            if L < 2:
                pe.wait_ge(weight_ready, 1)
                for b in range(B):
                    op = pe.transpose(weightT_ps[:, b // 4, (b % 4) * S:(b % 4 + 1) * S], R["weight"][:, b, :],
                                      ident[0:S, 0:S])
                op.then_inc(weightT_ready, 1)
                pe.wait_ge(weightT_kept, 1)
                for b in range(0, B, 2):
                    if b >= 4:
                        pe.wait_ge(bias_added, b // 2 - 1)
                    for j in range(2):
                        op = pe.matmul(bias_ps[:, b // 2 % 2, j * D:(j + 1) * D],
                                       weightT[:, (b + j) // 4, ((b + j) % 4) * S:((b + j) % 4 + 1) * S],
                                       b2[:, :], start=True, stop=True)
                    op.then_inc(bias_ready, 1)
            if L == 3:
                pe.wait_ge(first_ready, 1)
                pe.matmul(upto_ps[:, :], upto[:, :], first[:, :, :].rearrange("p b e -> p (b e)"), start=True, stop=True)\
                    .then_inc(counted, 1)

        @block.scalar
        def _(act):
            if L != 2:
                act.wait_ge(shifted_ready, 1)
                if L == 0:
                    act.activation(share2[:, :], top2[:, :], ACT.Exp).then_inc(exp_ready, 1)
                else:
                    act.activation(logits[:, :, :], logits[:, :, :], ACT.Exp).then_inc(exp_ready, 1)

        @block.vector
        def _(dve):
            count = [0]

            def then(op):
                count[0] += 1
                op.then_inc(step_done, 1)
                dve.wait_ge(step_done, count[0])

            def first_largest(out, values, largest):
                then(dve.tensor_reduce(largest[:, :], values, AX.X, ALU.max))
                then(dve.tensor_tensor(equal[:, :, :], values, over(largest[:, :]), ALU.is_equal))
                then(dve.tensor_tensor(equal[:, :, :], equal[:, :, :], rows(reverse[:, :]), ALU.mult))
                then(dve.tensor_reduce(rank[:, :], equal[:, :, :], AX.X, ALU.max))
                then(dve.tensor_tensor(out, equal[:, :, :], over(rank[:, :]), ALU.is_equal))

            if L == 2:
                dve.memset(chosen[:, :, :], 0).then_inc(cleared, 1)
                dve.memset(given[:, :, :], 0.0).then_inc(cleared, 1)
            dve.wait_ge(loaded, 16 * len(loads))
            values = logits[:, :, :]
            if L != 2:
                dve.wait_ge(logits_ready, 1)
                source = logits_ps[:, :].rearrange("p (b e) -> p b e", e=E)
                if L < 2:
                    then(dve.tensor_tensor(values, source, rows(gate_b[:, :]), ALU.add))
                else:
                    then(dve.tensor_copy(values, source))
            if L in (1, 3):
                then(dve.tensor_reduce(top[:, :], values, AX.X, ALU.max))
                dve.tensor_tensor(values, values, over(top[:, :]), ALU.subtract).then_inc(shifted_ready, 1)
                dve.wait_ge(exp_ready, 1)
                then(dve.tensor_reduce(share[:, :], values, AX.X, ALU.add))
                then(dve.reciprocal(share[:, :], share[:, :]))
                then(dve.tensor_tensor(values, values, over(share[:, :]), ALU.mult))
            if L != 2:
                first_largest(first[:, :, :], values, top)
            if L < 2:
                then(dve.scalar_tensor_tensor(values, first[:, :, :], -BIG, values, ALU.mult, ALU.add))
                first_largest(second[:, :, :], values, top2)
                one, two = top, top2
                if L == 0:
                    dve.tensor_tensor(top2[:, :], top2[:, :], top[:, :], ALU.subtract).then_inc(shifted_ready, 1)
                    dve.wait_ge(exp_ready, 1)
                    then(dve.tensor_scalar(share[:, :], share2[:, :], 1.0, None, ALU.add))
                    then(dve.reciprocal(share[:, :], share[:, :]))
                    then(dve.tensor_tensor(share2[:, :], share2[:, :], share[:, :], ALU.mult))
                    one, two = share, share2
                then(dve.tensor_tensor(first[:, :, :], first[:, :, :], over(one[:, :]), ALU.mult))
                then(dve.tensor_tensor(second[:, :, :], second[:, :, :], over(two[:, :]), ALU.mult))
            if L == 2:
                then(dve.tensor_copy(chosen_f[:, :, :], chosen[:, :, :]))
                for out, k in ((first, 0), (second, 1)):
                    then(dve.tensor_tensor(out[:, :, :], rows(expert[:, :]), over(chosen_f[:, :, k]), ALU.is_equal))
                    then(dve.tensor_tensor(out[:, :, :], out[:, :, :], over(given[:, :, k]), ALU.mult))
            tanh = G["tanh"][0:S, 4 + L:5 + L]
            if L < 3:
                then(dve.tensor_tensor(first[:, :, :], first[:, :, :], second[:, :, :], ALU.add))
                then(dve.tensor_scalar(R["weight"][:, :, :], first[:, :, :], tanh, None, ALU.mult))
            if L < 2:
                dve.sem_inc(weight_ready, 1)
                dve.wait_ge(weightT_ready, 1)
                dve.tensor_copy(weightT[:, :, :], weightT_ps[:, :, 0:4 * S]).then_inc(weightT_kept, 1)
                for b in range(0, B, 2):
                    dve.wait_ge(bias_ready, b // 2 + 1)
                    entries = G["x"][:, b:b + 2, :]
                    dve.tensor_tensor(entries, bias_ps[:, b // 2 % 2, :].rearrange("p (b d) -> p b d", b=2), entries,
                                      ALU.add).then_inc(bias_added, 1)
            if L == 2:
                then(dve.tensor_scalar(bias[:, :], bias[:, :], tanh, None, ALU.mult))
                then(dve.tensor_tensor(G["x"][:, :, :], G["x"][:, :, :],
                                       bias[:, :].unsqueeze(1).broadcast_to([S, B, D]), ALU.add))
            if L == 3:
                dve.sem_inc(first_ready, 1)
                dve.wait_ge(counted, 1)
                then(dve.tensor_tensor(place[:, :, :], upto_ps[:, :].rearrange("p (b e) -> p b e", e=E), first[:, :, :],
                                       ALU.mult))
                then(dve.tensor_scalar(place[:, :, :], place[:, :, :], -1.0, None, ALU.add))
                be = [S, B * E, CAP]
                then(dve.tensor_tensor(R["slots"][:, :, :].rearrange("p b (e c) -> p (b e) c", e=E),
                                       slot[:, :].unsqueeze(1).broadcast_to(be),
                                       place[:, :, :].rearrange("p b e -> p (b e)").unsqueeze(2).broadcast_to(be),
                                       ALU.is_equal))
                then(dve.tensor_scalar(R["gate"][:, :], top[:, :], tanh, None, ALU.mult))


def load_matrices(eng, A, L, matrices, e, par):
    for n in range(matrices["ups"]):
        eng.dma_start(matrices["up"][:, par, n, :, :], A[f"L{L}_up{n}"][bass.ds(e, 1), :, :, :])\
            .then_inc(matrices["loaded"][par], 16)
    eng.dma_start(matrices["down"][:, par, :, :], A[f"L{L}_down"][bass.ds(e, 1), :, :, :])\
        .then_inc(matrices["loaded"][par], 16)


def mixture(nc, A, G, L):
    ups, H = 2 if L == 0 else 1, 512 if L < 2 else 1024
    with ExitStack() as stack:
        sb, _, sem = makers(nc, stack)
        matrices = {"ups": ups, "up": sb(f"up{L}", [128, 2, ups, KD, H]), "down": sb(f"down{L}", [128, 2, H // 128, D]),
                    "loaded": [sem(f"matrices_loaded{L}_{par}") for par in range(2)]}
        for e in range(2):
            load_matrices(nc.sync, A, L, matrices, e, e)
        if L < 3:
            R = {"weight": sb(f"weight{L}", [S, B, E])}
            layernorm_transposed(nc, G, f"m{L}")
            route(nc, A, G, L, R)
            experts(nc, A, G, L, R, matrices)
        else:
            R = {"slots": sb("slots", [S, B, SLOTS]), "gate": sb("gate", [S, B])}
            natural = sb("natural", [S, B, D])
            layernorm_transposed(nc, G, "m3", natural=natural)
            route(nc, A, G, L, R)
            experts_with_slots(nc, A, G, R, natural, matrices)


def experts(nc, A, G, L, R, matrices):
    H = 1024 if L == 2 else 512
    J = H // 128
    ENTRIES = -(-T2 // S) if L == 2 else B
    tokens = [min(S, T2 - b * S) if L == 2 else S for b in range(ENTRIES)]
    chunks = [range(b, min(b + 4, ENTRIES)) for b in range(0, ENTRIES, 4)]
    UPS, UNITS = (2, len(chunks) * J) if L == 0 else (1, len(chunks) * J)
    SLOT = 2 if L == 0 else 4
    x, xnT = G["x"], G["xnT"]
    with ExitStack() as stack:
        sb0, ps0, sem0 = makers(nc, stack)

        def sb(name, shape):
            return sb0(f"e{L}_{name}", shape, F32)

        up, down, matrices_loaded = matrices["up"], matrices["down"], matrices["loaded"]
        up_bias = sb("up_bias", [128, UPS, E, J]) if L < 2 else None
        bias_now = sb("bias_now", [128, 2, UPS, J]) if L < 2 else None
        weight_now = sb("weight_now", [S, 2, B])
        hidden = sb("hidden", [128, 2, J, 4 * S])
        silu = sb("silu", [128, 2, 4 * S]) if L == 0 else None
        up_ps = ps0(f"e{L}_up_ps", [128, SLOT, UPS, 512])
        down_ps = ps0(f"e{L}_down_ps", [S, 4, 512])
        biases_loaded = sem0(f"e{L}_biases_loaded")
        up_filled = Signal(sem0(f"e{L}_up_filled"), UNITS, lead=1)
        silu_ready = Signal(sem0(f"e{L}_silu_ready"), UNITS, lead=1)
        hidden_ready = Signal(sem0(f"e{L}_hidden_ready"), UNITS, lead=1)
        down_filled = Signal(sem0(f"e{L}_down_filled"), ENTRIES, lead=1)
        x_added = Signal(sem0(f"e{L}_x_added"), ENTRIES, lead=1)
        picked = Signal(sem0(f"e{L}_picked"), 1, lead=1)
        LOADS = UPS + 1
        block = stack.enter_context(nc.Block())

        def all_experts(eng, body):
            with eng.Fori(0, E // 2) as i:
                for par in range(2):
                    body(i * 2 + par, par)

        @block.sync
        def _(sp):
            if L < 2:
                for n in range(UPS):
                    sp.dma_start(up_bias[:, n, :, :], A[f"L{L}_up_bias{n}"]).then_inc(biases_loaded, 16)
            with sp.Fori(0, E // 2 - 1) as i:
                for par in range(2):
                    e = i * 2 + par
                    sp.wait_ge(down_filled.sem, down_filled.at(e, ENTRIES - 1))
                    load_matrices(sp, A, L, matrices, e + 2, par)

        @block.tensor
        def _(pe):
            up_filled.credit(pe)
            down_filled.credit(pe)

            def fill_up(e, par, c):
                chunk = chunks[c]
                t0, n = chunk[0] * S, sum(tokens[b] for b in chunk)
                for j in range(J):
                    u = c * J + j
                    pe.wait_ge(hidden_ready.sem, hidden_ready.at(e, u - SLOT) if u >= SLOT
                               else hidden_ready.at(e - 1, u - SLOT + UNITS))
                    for m in range(UPS):
                        for k in range(KD):
                            op = pe.matmul(up_ps[:, u % SLOT, m, 0:n], up[:, par, m, k, j * 128:(j + 1) * 128],
                                           xnT[:, k, t0:t0 + n], start=k == 0, stop=k == KD - 1)
                    op.then_inc(up_filled.sem, 1)

            def fill_down(e, par, c):
                pe.wait_ge(hidden_ready.sem, hidden_ready.at(e, c * J + J - 1))
                for r, b in enumerate(chunks[c]):
                    before = (e, b - 4) if b >= 4 else (e - 1, max(m for m in range(ENTRIES) if m % 4 == b % 4))
                    pe.wait_ge(x_added.sem, x_added.at(*before))
                    for j in range(J):
                        op = pe.matmul(down_ps[0:tokens[b], b % 4, 0:D], hidden[:, c % 2, j, r * S:r * S + tokens[b]],
                                       down[:, par, j, :], start=j == 0, stop=j == J - 1)
                    op.then_inc(down_filled.sem, 1)

            def body(e, par):
                pe.wait_ge(matrices_loaded[par], e * (8 * LOADS) + (16 - 8 * par) * LOADS)
                fill_up(e, par, 0)
                for c in range(len(chunks)):
                    if c + 1 < len(chunks):
                        fill_up(e, par, c + 1)
                    fill_down(e, par, c)

            all_experts(pe, body)

        @block.scalar
        def _(act):
            (silu_ready if L == 0 else hidden_ready).credit(act)

            def body(e, par):
                if L < 2:
                    act.wait_ge(picked.sem, picked.at(e))
                for c, chunk in enumerate(chunks):
                    n = sum(tokens[b] for b in chunk)
                    for j in range(J):
                        u = c * J + j
                        act.wait_ge(up_filled.sem, up_filled.at(e, u))
                        if L == 0:
                            act.wait_ge(hidden_ready.sem, hidden_ready.at(e, u - 2) if u >= 2
                                        else hidden_ready.at(e - 1, u - 2 + UNITS))
                            act.activation(silu[:, u % 2, 0:n], up_ps[:, u % SLOT, 1, 0:n], ACT.Silu,
                                           bias=bias_now[:, par, 1, j:j + 1]).then_inc(silu_ready.sem, 1)
                        else:
                            bias = bias_now[:, par, 0, j:j + 1] if L == 1 else 0.0
                            act.activation(hidden[:, c % 2, j, 0:n], up_ps[:, u % SLOT, 0, 0:n],
                                           ACT.Relu if L == 1 else ACT.Gelu, bias=bias).then_inc(hidden_ready.sem, 1)

            all_experts(act, body)

        @block.vector
        def _(dve):
            x_added.credit(dve)
            picked.credit(dve)
            if L == 0:
                hidden_ready.credit(dve)
            if L < 2:
                dve.wait_ge(biases_loaded, 16 * UPS)

            def gate_hidden(e, par, c):
                n = 4 * S
                for j in range(J):
                    u = c * J + j
                    dve.wait_ge(silu_ready.sem, silu_ready.at(e, u))
                    dve.scalar_tensor_tensor(hidden[:, c % 2, j, 0:n], up_ps[:, u % SLOT, 0, 0:n],
                                             bias_now[:, par, 0, j:j + 1], silu[:, u % 2, 0:n], ALU.add, ALU.mult)\
                        .then_inc(hidden_ready.sem, 1)

            def add(e, par, c):
                for b in chunks[c]:
                    n = tokens[b]
                    dve.wait_ge(down_filled.sem, down_filled.at(e, b))
                    dve.scalar_tensor_tensor(x[0:n, b, :], down_ps[0:n, b % 4, 0:D], weight_now[0:n, par, b:b + 1],
                                             x[0:n, b, :], ALU.mult, ALU.add).then_inc(x_added.sem, 1)

            def body(e, par):
                if L < 2:
                    dve.wait_ge(hidden_ready.sem, hidden_ready.at(e - 1, UNITS - 1))
                    dve.tensor_copy(bias_now[:, par, :, :].unsqueeze(2), up_bias[:, :, bass.ds(e, 1), :])
                dve.wait_ge(x_added.sem, x_added.at(e - 1, ENTRIES - 1))
                dve.tensor_copy(weight_now[:, par, :].unsqueeze(2), R["weight"][:, :, bass.ds(e, 1)]).then_inc(picked.sem, 1)
                dve.wait_ge(picked.sem, picked.at(e))
                if L == 0:
                    gate_hidden(e, par, 0)
                for c in range(len(chunks)):
                    if L == 0 and c + 1 < len(chunks):
                        gate_hidden(e, par, c + 1)
                    add(e, par, c)

            all_experts(dve, body)


def experts_with_slots(nc, A, G, R, natural, matrices):
    H, ROWS, HALF = 1024, B * CAP, B * CAP // 2
    J = H // 128
    x, ident = G["x"], G["ident"]
    slots = R["slots"]
    with ExitStack() as stack:
        sb0, ps0, sem0 = makers(nc, stack)

        def sb(name, shape):
            return sb0(f"e3_{name}", shape, F32)

        up, down, matrices_loaded = matrices["up"], matrices["down"], matrices["loaded"]
        takenT = sb("takenT", [128, KD, E, ROWS])
        slotsT = sb("slotsT", [SLOTS, B, S])
        hidden = sb("hidden", [128, J, ROWS])
        answers = sb("answers", [HALF, 2, 2, D])
        regrouped = sb("regrouped", [SLOTS, B, D])
        taken_ps = ps0("e3_taken_ps", [128, 2, 512])
        turned_ps = ps0("e3_turned_ps", [SLOTS, 2, 512])
        up_ps = ps0("e3_up_ps", [128, 2, 512])
        down_ps = ps0("e3_down_ps", [HALF, 2, 2 * D])
        scratch = nc.dram_tensor("answers_dram", (E, B, CAP, D), F32, kind="Internal").ap()
        taken_filled = sem0("e3_taken_filled")
        taken_kept = sem0("e3_taken_kept")
        turned_filled = sem0("e3_turned_filled")
        turned_kept = sem0("e3_turned_kept")
        PAIRS = J // 2
        up_filled = Signal(sem0("e3_up_filled"), PAIRS, lead=1)
        hidden_ready = Signal(sem0("e3_hidden_ready"), PAIRS, lead=1)
        down_filled = Signal(sem0("e3_down_filled"), 1, lead=2)
        answer_kept = Signal(sem0("e3_answer_kept"), 1, lead=2)
        stored = [sem0(f"e3_stored{par}") for par in range(2)]
        regrouped_loaded = sem0("e3_regrouped_loaded")
        mixed_filled = sem0("e3_mixed_filled")
        x_added = sem0("e3_x_added")
        block = stack.enter_context(nc.Block())

        def all_experts(eng, body):
            with eng.Fori(0, E // 2) as i:
                for par in range(2):
                    body(i * 2 + par, par)

        @block.sync
        def _(sp):
            with sp.Fori(0, E // 2 - 1) as i:
                for par in range(2):
                    e = i * 2 + par
                    sp.wait_ge(down_filled.sem, down_filled.at(e))
                    load_matrices(sp, A, 3, matrices, e + 2, par)
            for par in range(2):
                sp.wait_ge(stored[par], 16 * E // 2)
            for e in range(E):
                sp.dma_start(regrouped[e * CAP:(e + 1) * CAP, :, :], scratch[e].rearrange("b c d -> c b d"))\
                    .then_inc(regrouped_loaded, 16)

        @block.gpsimd
        def _(pool):
            def body(e, par):
                pool.wait_ge(answer_kept.sem, answer_kept.at(e))
                out = scratch[bass.ds(e, 1), :, :, :].rearrange("a (h b) c d -> (a b c) h d", h=2)
                pool.dma_start(out, answers[:, par, :, :]).then_inc(stored[par], 16)

            all_experts(pool, body)

        @block.tensor
        def _(pe):
            up_filled.credit(pe)
            down_filled.credit(pe)
            for b in range(B):
                if b >= 2:
                    pe.wait_ge(taken_kept, b - 1)
                for k in range(KD):
                    op = pe.matmul(taken_ps[:, b % 2, k * SLOTS:(k + 1) * SLOTS], natural[:, b, k * 128:(k + 1) * 128],
                                   slots[:, b, :], start=True, stop=True)
                op.then_inc(taken_filled, 1)
                if b >= 2:
                    pe.wait_ge(turned_kept, b - 1)
                pe.transpose(turned_ps[:, b % 2, 0:S], slots[:, b, :], ident[0:S, 0:S]).then_inc(turned_filled, 1)
            pe.wait_ge(taken_kept, B)

            def body(e, par):
                pe.wait_ge(matrices_loaded[par], e * 16 + 32 - 16 * par)
                for u in range(PAIRS):
                    pe.wait_ge(hidden_ready.sem, hidden_ready.at(e, u - 2) if u >= 2
                               else hidden_ready.at(e - 1, u - 2 + PAIRS))
                    for j in (2 * u, 2 * u + 1):
                        for k in range(KD):
                            op = pe.matmul(up_ps[:, u % 2, (j % 2) * ROWS:(j % 2 + 1) * ROWS],
                                           up[:, par, 0, k, j * 128:(j + 1) * 128],
                                           takenT[:, k, bass.ds(e, 1), :], start=k == 0, stop=k == KD - 1)
                    op.then_inc(up_filled.sem, 1)
                pe.wait_ge(answer_kept.sem, answer_kept.at(e - 2))
                pe.wait_ge(hidden_ready.sem, hidden_ready.at(e, PAIRS - 1))
                for half in range(2):
                    for j in range(J):
                        op = pe.matmul(down_ps[:, par, half * D:(half + 1) * D], hidden[:, j, half * HALF:(half + 1) * HALF],
                                       down[:, par, j, :], start=j == 0, stop=j == J - 1)
                op.then_inc(down_filled.sem, 1)

            all_experts(pe, body)
            pe.wait_ge(regrouped_loaded, 16 * E)
            pe.wait_ge(turned_kept, B)
            for b in range(B):
                if b >= 2:
                    pe.wait_ge(x_added, b - 1)
                pe.matmul(taken_ps[0:S, b % 2, 0:D], slotsT[:, b, :], regrouped[:, b, :], start=True, stop=True)\
                    .then_inc(mixed_filled, 1)

        @block.scalar
        def _(act):
            hidden_ready.credit(act)
            for b in range(B):
                act.wait_ge(taken_filled, b + 1)
                act.activation(takenT[:, :, :, b * CAP:(b + 1) * CAP],
                               taken_ps[:, b % 2, 0:KD * SLOTS].rearrange("p (k e c) -> p k e c", k=KD, e=E),
                               ACT.Copy).then_inc(taken_kept, 1)

            def body(e, par):
                act.wait_ge(down_filled.sem, down_filled.at(e - 1))
                for u in range(PAIRS):
                    act.wait_ge(up_filled.sem, up_filled.at(e, u))
                    act.activation(hidden[:, 2 * u:2 * u + 2, :], up_ps[:, u % 2, 0:2 * ROWS], ACT.Gelu_apprx_tanh)\
                        .then_inc(hidden_ready.sem, 1)

            all_experts(act, body)

        @block.vector
        def _(dve):
            answer_kept.credit(dve)
            for b in range(B):
                dve.wait_ge(turned_filled, b + 1)
                dve.tensor_copy(slotsT[:, b, :], turned_ps[:, b % 2, 0:S]).then_inc(turned_kept, 1)

            def body(e, par):
                dve.wait_ge(down_filled.sem, down_filled.at(e))
                dve.tensor_copy(answers[:, par, :, :], down_ps[:, par, :]).then_inc(answer_kept.sem, 1)

            body(0, 0)
            body(1, 1)
            with dve.Fori(0, E // 2 - 1) as i:
                for par in range(2):
                    dve.wait_ge(stored[par], i * 16 + 16)
                    body(i * 2 + par + 2, par)
            for b in range(B):
                dve.wait_ge(mixed_filled, b + 1)
                dve.scalar_tensor_tensor(x[:, b, :], taken_ps[0:S, b % 2, 0:D], R["gate"][:, b:b + 1], x[:, b, :],
                                         ALU.mult, ALU.add).then_inc(x_added, 1)


def build(nc, A, out):
    with ExitStack() as stack:
        sb, _, sem = makers(nc, stack)
        G = {"x": sb("x", [S, B, D]), "xnT": sb("xnT", [128, KD, B * S]), "ident": sb("ident", [128, 128]),
             "headmask": sb("headmask", [128, 8]), "tanh": sb("tanh", [128, 8]),
             "key_mask": sb("key_mask", [S, B, C], U8), "query_on": sb("query_on", [S, B]),
             "ln_eps": sb("ln_eps", [S, 1]), "rms_eps": sb("rms_eps", [128, 1])}
        load_state(nc, A, G)
        for layer in range(4):
            attention(nc, A, G, layer)
            mixture(nc, A, G, layer)
        stored = sem("stored")
        block = stack.enter_context(nc.Block())

        @block.sync
        def _(sp):
            sp.dma_start(out.rearrange("b s d -> s b d"), G["x"][:, :, :]).then_inc(stored, 16)
            sp.wait_ge(stored, 16)


def laid_out(inputs):
    def tiles(w):
        return w.reshape(-1, 128, w.shape[1]).transpose(1, 0, 2)

    g = {k: np.asarray(a) for k, a in inputs.items()}
    A = {k: g[k] for k in ("x", "g_xattn", "g_ffn")}
    A["mask_BxS2_bk0"] = g["mask_BxS2_bk0"]
    A["mask_BxS_bk0T"] = g["mask_BxS_bk0"].T
    A["ctxT"] = g["ctx_1024"].reshape(B, C, KD, 128).transpose(0, 3, 2, 1)
    A["L0_xattn_wq"] = tiles(g["L0_xattn_Wq"])
    A["L0_xattn_wk"] = tiles(g["L0_xattn_Wkv"][:, :1024])
    A["L0_xattn_wv"] = tiles(g["L0_xattn_Wkv"][:, 1024:])
    A["L0_xattn_wo"] = tiles(g["L0_xattn_Wout"])
    A["L0_xattn_bo"] = g["L0_xattn_bout"]
    for L in (1, 3):
        for n in "qkvo":
            A[f"L{L}_xattn_w{n}"] = tiles(g[f"L{L}_xattn_W{n}"].T)
            b = g[f"L{L}_xattn_b{n}"]
            A[f"L{L}_xattn_b{n}"] = b.reshape(KD, 128).T if n in "qk" else b
    for n in "qkvo":
        A[f"L2_xattn_w{n}"] = tiles(g[f"L2_xattn_w{n}_w"])
    A["L2_xattn_bv"], A["L2_xattn_bo"] = g["L2_xattn_wv_b"], g["L2_xattn_wo_b"]
    for n in ("wq_b", "wk_b", "qn_w", "kn_w"):
        A[f"L2_xattn_{n}"] = g[f"L2_xattn_{n}"]
    A["ident"] = np.eye(128, dtype=np.float32)
    A["headmask"] = (np.arange(128)[:, None] // 16 == np.arange(8)).astype(np.float32)
    hd = 16
    inv_freq = 1.0 / 10000.0 ** (np.arange(0, hd, 2, dtype=np.float32) / np.float32(hd))
    pos = np.concatenate([np.arange(CP), np.arange(KP)]).astype(np.float32)
    angle = (pos[:, None] * inv_freq.astype(np.float32)[None, :]).astype(np.float32)
    rows = lambda a: a.reshape(KT + 1, KP, hd).transpose(1, 0, 2).astype(np.float32)
    A["cos"] = rows(np.concatenate([np.cos(angle), np.cos(angle)], 1))
    A["sin"] = rows(np.concatenate([-np.sin(angle), np.sin(angle)], 1))
    laid_out_mlps(g, A, tiles)
    return {k: np.ascontiguousarray(a) for k, a in A.items()}


def laid_out_mlps(g, A, tiles):
    def ups(w):
        return w.reshape(E, -1, 128, w.shape[2]).transpose(0, 2, 1, 3)

    def bias(b):
        return b.reshape(E, -1, 128).transpose(2, 0, 1)

    for L in (0, 1):
        A[f"L{L}_gate_w"] = tiles(g[f"L{L}_ffn_gate_w"].T)
        A[f"L{L}_ffn_gate_b"], A[f"L{L}_ffn_b2"] = g[f"L{L}_ffn_gate_b"], g[f"L{L}_ffn_b2"]
    A["L3_gate_w"] = tiles(g["L3_ffn_Wg"])
    for n in range(2):
        A[f"L0_up{n}"], A[f"L0_up_bias{n}"] = ups(g[f"L0_ffn_w{n}"].transpose(0, 2, 1)), bias(g[f"L0_ffn_b{n}"])
    A["L0_down"] = ups(g["L0_ffn_w2"].transpose(0, 2, 1))
    A["L1_up0"], A["L1_up_bias0"], A["L1_down"] = ups(g["L1_ffn_w1"]), bias(g["L1_ffn_b1"]), ups(g["L1_ffn_w2"])
    A["L2_up0"], A["L2_down"] = ups(g["L2_ffn_w1"]), ups(g["L2_ffn_w2"])
    A["L3_up0"], A["L3_down"] = ups(g["L3_ffn_W1"]), ups(g["L3_ffn_W2"])
    A["L2_indices"], A["L2_weights"] = g["L2_ffn_expert_indices"], g["L2_ffn_expert_weights"]
    A["L2_ffn_bias"] = g["L2_ffn_bias"]
    A["reverse"] = np.arange(E, 0, -1).astype(np.float32)
    A["expert"] = np.arange(E).astype(np.float32)
    A["slot"] = np.arange(CAP).astype(np.float32)
    A["upto"] = np.triu(np.ones((S, S), np.float32))


def kernel(**inputs):
    import concourse.bacc as _bacc
    from concourse.bass_utils import run_bass_kernel_spmd as _run

    nc = _bacc.Bacc("TRN2", target_bir_lowering=False, num_devices=1)
    arrays = laid_out(inputs)
    aps = {k: nc.dram_tensor(f"in_{k}", a.shape, mybir.dt.from_np(a.dtype), kind="ExternalInput").ap()
           for k, a in arrays.items()}
    out = nc.dram_tensor("out_0", (B, S, D), F32, kind="ExternalOutput").ap()
    build(nc, aps, out)
    r = _run(nc, [{f"in_{k}": a for k, a in arrays.items()}], core_ids=[0])
    return r.results[0]["out_0"]
```
